# Optimizing a Trainium2 kernel written in Bass

```python
import numpy as np
import jax
import jax.numpy as jnp

def _softmax(x, axis=-1):
    return jax.nn.softmax(x, axis=axis)

def _gelu(x):
    return jax.nn.gelu(x, approximate=True)

def _silu(x):
    return jax.nn.silu(x)

def _sigmoid(x):
    return jax.nn.sigmoid(x)

def _layernorm(x, axis=-1, eps=1e-05):
    m = jnp.mean(x, axis=axis, keepdims=True)
    v = jnp.var(x, axis=axis, keepdims=True)
    return (x - m) / jnp.sqrt(v + eps)

def _scatter_add(tgt, idx, src, axis=0):
    return tgt.at[idx].add(src)

def _segment_sum(src, seg, n):
    return jax.ops.segment_sum(src, seg, n)
kernel_name = 'mk_adj_ffn_d1_adj_r2_ece151'

def setup_inputs(seed: int=0):
    np.random.seed(seed)
    _w = jnp.asarray

    def _rec_inputs():
        import jax
        import jax.numpy as jnp
        _gk = jax.random.key(seed)
        x = -0.0005207 + 1.001 * jax.random.normal(jax.random.fold_in(_gk, 1), (4096, 128), jnp.float32)
        _a = jax.random.bernoulli(jax.random.fold_in(_gk, 2), 0.00195312, (4096, 4096))
        adj = _a.astype(jnp.int32)
        return (x, adj)
    x, adj = _rec_inputs()

    def _L0_gnn_setup():
        import jax, jax.numpy as jnp
        import numpy as np
        N, D, H = (4096, 128, 128)
        KEEP_RATIO = 0.5
        TEMP = 1.0
        COS_EPS = 0.0001
        NEG = -9000000000000000.0

        def _cos_normalize(x):
            n = jnp.linalg.norm(x, axis=-1, keepdims=True)
            return x / jnp.maximum(n, COS_EPS)
        key = jax.random.key(seed)
        k1, k2, k3, k4 = jax.random.split(key, 4)
        features = jax.random.normal(k1, (N, D), dtype=jnp.float32)
        adj = jax.random.randint(k2, (N, N), 0, 2, dtype=jnp.int32)
        Wq = jax.random.normal(k3, (H, D), dtype=jnp.float32) * 0.001
        Wk = jax.random.normal(k4, (H, D), dtype=jnp.float32) * 0.001
        return {'features': features, 'adj': adj, 'Wq': Wq, 'Wk': Wk}
    _L0_gnn_all = _L0_gnn_setup()
    _L0_gnn_in = {k: v for k, v in _L0_gnn_all.items() if k in ('Wq', 'Wk')}
    del _L0_gnn_all

    def _L0_ffn_setup():
        import jax, jax.numpy as jnp
        import numpy as np
        D_MODEL = 128
        EXPERT_DIM = 256
        NUM_EXPERTS = 8
        TOP_K = 2
        SEQ_LEN = 1024
        BATCH = 2
        key = jax.random.key(seed)
        ks = jax.random.split(key, 8)
        s = 0.02
        x = jax.random.normal(ks[0], (SEQ_LEN, BATCH, D_MODEL), dtype=jnp.float32)
        Wg = jax.random.normal(ks[1], (D_MODEL, NUM_EXPERTS), dtype=jnp.float32) * s
        bg = jax.random.normal(ks[2], (NUM_EXPERTS,), dtype=jnp.float32) * s
        bias = jnp.zeros((NUM_EXPERTS,), dtype=jnp.float32)
        W1 = jax.random.normal(ks[3], (NUM_EXPERTS, D_MODEL, EXPERT_DIM), dtype=jnp.float32) * s
        b1 = jax.random.normal(ks[4], (NUM_EXPERTS, EXPERT_DIM), dtype=jnp.float32) * s
        W2 = jax.random.normal(ks[5], (NUM_EXPERTS, EXPERT_DIM, D_MODEL), dtype=jnp.float32) * s
        b2 = jax.random.normal(ks[6], (NUM_EXPERTS, D_MODEL), dtype=jnp.float32) * s
        return {'x': x, 'Wg': Wg, 'bg': bg, 'bias': bias, 'W1': W1, 'b1': b1, 'W2': W2, 'b2': b2}
    _L0_ffn_all = _L0_ffn_setup()
    _L0_ffn_in = {k: v for k, v in _L0_ffn_all.items() if k in ('Wg', 'bg', 'bias', 'W1', 'b1', 'W2', 'b2')}
    del _L0_ffn_all
    return {'x': x, 'adj': adj, 'L0_gnn_Wq': _L0_gnn_in['Wq'], 'L0_gnn_Wk': _L0_gnn_in['Wk'], 'L0_ffn_Wg': _L0_ffn_in['Wg'], 'L0_ffn_bg': _L0_ffn_in['bg'], 'L0_ffn_bias': _L0_ffn_in['bias'], 'L0_ffn_W1': _L0_ffn_in['W1'], 'L0_ffn_b1': _L0_ffn_in['b1'], 'L0_ffn_W2': _L0_ffn_in['W2'], 'L0_ffn_b2': _L0_ffn_in['b2']}

def reference(x, adj, L0_gnn_Wq, L0_gnn_Wk, L0_ffn_Wg, L0_ffn_bg, L0_ffn_bias, L0_ffn_W1, L0_ffn_b1, L0_ffn_W2, L0_ffn_b2):
    import jax
    import jax.numpy as jnp

    def _L0_gnn_ref(features, adj, Wq, Wk):
        import jax, jax.numpy as jnp
        import numpy as np
        N, D, H = (4096, 128, 128)
        KEEP_RATIO = 0.5
        TEMP = 1.0
        COS_EPS = 0.0001
        NEG = -9000000000000000.0

        def _cos_normalize(x):
            n = jnp.linalg.norm(x, axis=-1, keepdims=True)
            return x / jnp.maximum(n, COS_EPS)
        Qn = _cos_normalize(features @ Wq.T)
        Kn = _cos_normalize(features @ Wk.T)
        raw_att = Kn @ Qn.T
        att = jnp.where(adj > 0, raw_att, NEG) * TEMP
        att = jax.nn.softmax(att, axis=1)
        prop_fea = att @ features
        adj_mask = (jnp.sum(adj, axis=1) > 0).astype(features.dtype)[:, None]
        prop_fea = adj_mask * prop_fea + (1.0 - adj_mask) * features
        return (1.0 - KEEP_RATIO) * prop_fea + KEEP_RATIO * features

    def _L0_ffn_ref(x, Wg, bg, bias, W1, b1, W2, b2):
        import jax, jax.numpy as jnp
        import numpy as np
        D_MODEL = 128
        EXPERT_DIM = 256
        NUM_EXPERTS = 8
        TOP_K = 2
        SEQ_LEN = 1024
        BATCH = 2
        x_flat = x.reshape(-1, D_MODEL)
        gate_logits = x_flat @ Wg + bg + bias
        topk_vals, topk_idx = jax.lax.top_k(gate_logits, TOP_K)
        topk_w = jax.nn.softmax(topk_vals, axis=-1)
        combine = (jax.nn.one_hot(topk_idx, NUM_EXPERTS, dtype=x.dtype) * topk_w[..., None]).sum(axis=1)
        h = jax.nn.relu(jnp.einsum('td,edh->teh', x_flat, W1) + b1)
        y = jnp.einsum('teh,ehd->ted', h, W2) + b2
        out = jnp.einsum('ted,te->td', y, combine)
        return out.reshape(x.shape)
    x = x + _L0_gnn_ref(_layernorm(x, axis=-1), adj, L0_gnn_Wq, L0_gnn_Wk)
    x = x + _L0_ffn_ref(_layernorm(x, axis=-1)[None], L0_ffn_Wg, L0_ffn_bg, L0_ffn_bias, L0_ffn_W1, L0_ffn_b1, L0_ffn_W2, L0_ffn_b2)[0]
    return x

_drawn_inputs = setup_inputs


def setup_inputs(seed=0):
    import zlib

    import numpy as np

    out = dict(_drawn_inputs(seed))
    spreads = {'L0_ffn_bias': (0.0, 0.418)}
    factors = {'L0_gnn_Wq': 25.468,
     'L0_gnn_Wk': 25.715,
     'L0_ffn_bg': 8.0,
     'L0_ffn_W1': 2.852,
     'L0_ffn_b1': 28.162,
     'L0_ffn_b2': 5.85}
    for name, (base, spread) in spreads.items():
        noise = np.random.default_rng([zlib.crc32(name.encode()), seed]).standard_normal(out[name].shape)
        drawn = base * np.exp(spread * noise) if base else spread * noise
        out[name] = jnp.asarray(drawn.astype(out[name].dtype))
    for name, factor in factors.items():
        out[name] = (out[name] * factor).astype(out[name].dtype)
    return out
```

```python
from contextlib import ExitStack

import concourse.bass as bass
from concourse import mybir

F32 = mybir.dt.float32
F16 = mybir.dt.float16
BF16 = mybir.dt.bfloat16
I32 = mybir.dt.int32
ALU = mybir.AluOpType
ACT = mybir.ActivationFunctionType
AX_X = mybir.AxisListType.X

P = 128
SUB = 4
PAIR = 2
LN_EPS = 1e-5
COS_EPS = 1e-4
W_SCALE = 64.0
UNIT_SCALE = 256.0
MASK = -float(2 ** 30)
TINY = 1e-30
UP = 1024.0


def gnn_moe_layer(nc, x, adj, Wq, Wk, Wg, bg, bias, W1, b1, W2, b2, out):
    N, D = x.shape
    E_N, _, F = W1.shape
    T = N // P
    CH = SUB * P
    C = N // CH
    J = N // P
    S = J // PAIR
    SW = PAIR * P
    QS = 4
    QW = QS * SW
    NQ = N // QW
    FB = F // P
    SC = 1.0 / (UNIT_SCALE * UNIT_SCALE)

    with ExitStack() as ctx:
        def sb(name, shape, dt):
            return ctx.enter_context(nc.sbuf_tensor(name, shape, dt))

        def ps(name, shape, dt):
            return ctx.enter_context(nc.psum_tensor(name, shape, dt))

        def sem(name):
            return ctx.enter_context(nc.semaphore(name))

        base = sb("base", [P, T, D], F32)
        xn = sb("xn", [P, T, D], F32)
        xa = sb("xa", [P, T, D + 1], F16)
        xl = sb("xl", [P, T, D], BF16)
        kqh = sb("kqh", [P, 2, N], F16)
        kql = sb("kql", [P, 2, N], BF16)
        noedge = sb("noedge", [P, SUB, N], BF16)
        adj_in = sb("adj_in", [P, 2, SUB, QW], I32)
        e_f = sb("e_f", [P, 2, PAIR * CH], F32)
        e_h = sb("e_h", [P, 2, PAIR * CH], F16)
        e_l = sb("e_l", [P, 2, PAIR * CH], BF16)
        w1h = sb("w1h", [P, E_N * F], F16)
        w1l = sb("w1l", [P, E_N * F], BF16)
        w2h = sb("w2h", [P, E_N * FB * D], F16)
        w2l = sb("w2l", [P, E_N * FB * D], BF16)
        w1_in = sb("w1_in", [P, E_N * F], F32)
        w2_in = kqh[:, 1, :].bitcast(F32)
        wkq_in = sb("wkq_in", [P, 2, D], F32)
        wkqh = sb("wkqh", [P, 2 * D], F16)
        wkql = sb("wkql", [P, 2 * D], BF16)
        wg = sb("wg", [P, E_N], F32)
        gb = sb("gb", [P, 2, E_N], F32)
        b1_in = sb("b1_in", [E_N * FB, P], F32)
        b1c = sb("b1c", [P, E_N * FB], F32)
        b2s = sb("b2s", [E_N, D], F32)
        ident = sb("ident", [P, P], F32)
        ident_h = sb("ident_h", [P, P], F16)
        ident_b = sb("ident_b", [P, P], BF16)
        mask_i = sb("mask_i", [P, P], BF16)
        half = sb("half", [P, T], F32)
        st = sb("st", [P, T, 6], F32)
        mv = sb("mv", [P, T, 2], F32)
        veps = sb("veps", [P, T], F32)
        rstd = sb("rstd", [P, T], F32)
        xc = sb("xc", [P, 2, SUB, D], F32)
        xth = sb("xth", [P, 2, CH], F16)
        xtl = sb("xtl", [P, 2, CH], BF16)
        kq, sq = e_f, w1_in[:].rearrange("p (u n) -> p u n", u=2)
        kch = e_h[:].rearrange("p u (s k d) -> p u s k d", k=2, d=D)
        kcl = e_l[:].rearrange("p u (s k d) -> p u s k d", k=2, d=D)
        ss = sb("ss", [P, 2, SUB * 2], F32)
        rn = sb("rn", [P, 2, SUB * 2], F32)
        den = sb("den", [P, SUB], F32)
        rden = sb("rden", [P, SUB], F32)
        alone = sb("alone", [P, SUB], F32)
        mx_t = sb("mx_t", [P, SUB, D], F32)
        rank = sb("rank", [P, SUB, E_N], F32)
        lg = sb("lg", [P, SUB, E_N], F32)
        lg2 = sb("lg2", [P, SUB, E_N], F32)
        cand = sb("cand", [P, SUB, E_N], F32)
        oh1 = sb("oh1", [P, SUB, E_N], F32)
        oh2 = sb("oh2", [P, SUB, E_N], F32)
        top = sb("top", [P, 4, SUB], F32)
        gw = sb("gw", [P, 4, SUB], F32)
        cw = sb("cw", [P, T, E_N], F32)
        cfull = sb("cfull", [P, SUB, E_N], F32)
        ct = sb("ct", [E_N, CH], F32)
        xtf = sb("xtf", [P, CH], F32)

        ps_s = ps("ps_s", [P, 2, PAIR * CH], F32)
        ps_o = ps("ps_o", [P, SUB, 2 * P], F32)
        ps_a = ps("ps_a", [P, CH], F32)
        ps_b = ps("ps_b", [P, CH], F32)

        s_x = sem("s_x")
        s_w = sem("s_w")
        s_w1 = sem("s_w1")
        s_adj = [sem("s_adj0"), sem("s_adj1")]
        s_out = sem("s_out")
        k_set = sem("k_set")
        k_id = sem("k_id")
        wt_ps = sem("wt_ps")
        wt_h = sem("wt_h")
        wt_l = sem("wt_l")
        st_ok = sem("st_ok")
        rs_ok = sem("rs_ok")
        xn_ok = sem("xn_ok")
        xn_kept = sem("xn_kept")
        xh_ok = sem("xh_ok")
        xt_ps = sem("xt_ps")
        xth_ok = sem("xth_ok")
        xtl_ok = sem("xtl_ok")
        kq_ps = sem("kq_ps")
        kq_ok = sem("kq_ok")
        ss_ok = sem("ss_ok")
        rn_ok = sem("rn_ok")
        kn_ok = sem("kn_ok")
        kch_ok = sem("kch_ok")
        kcl_ok = sem("kcl_ok")
        kt_ps = sem("kt_ps")
        kth_ok = sem("kth_ok")
        ktl_ok = sem("ktl_ok")
        conv = sem("conv")
        s_ps = sem("s_ps")
        e_ok = sem("e_ok")
        eh_ok = sem("eh_ok")
        el_ok = sem("el_ok")
        pv = sem("pv")
        o_free = sem("o_free")
        l2_st = sem("l2_st")
        l2_rs = sem("l2_rs")
        l2_x = sem("l2_x")
        l2_ps = sem("l2_ps")
        l2_f = sem("l2_f")
        l2_h = sem("l2_h")
        l2_l = sem("l2_l")
        g_ps = sem("g_ps")
        g_d = sem("g_d")
        g_e = sem("g_e")
        c_ok = sem("c_ok")
        ct_ps = sem("ct_ps")
        ct_ok = sem("ct_ok")
        b2_ps = sem("b2_ps")
        b2_ok = sem("b2_ok")
        z_ps = sem("z_ps")
        h_ok = sem("h_ok")
        hh_ok = sem("hh_ok")
        hl_ok = sem("hl_ok")
        y_ps = sem("y_ps")
        y_ok = sem("y_ok")
        y_acc = sem("y_acc")

        x2h, x2l = kqh[:, 0, :], kql[:, 0, :]

        block = ctx.enter_context(nc.Block())

        @block.sync
        def _(sp):
            sp.dma_start(base[:, :, :], x.rearrange("(t p) d -> p t d", p=P)).then_inc(s_x, 16)

            def load_adj(c, q, b):
                sp.dma_start(adj_in[:, b, :, :],
                             adj.rearrange("(c s p) (q w) -> c q p s w", s=SUB, p=P, w=QW)[c, q]
                             ).then_inc(s_adj[b], 16)
            load_adj(0, 0, 0)
            load_adj(0, 1, 1)
            for q in range(2, NQ):
                sp.wait_ge(conv, QS * (q - 1))
                load_adj(0, q, q % 2)
            with sp.Fori(1, C) as c:
                for q in range(NQ):
                    sp.wait_ge(conv, c * S + QS * (q - 1))
                    load_adj(c, q, q % 2)
            sp.wait_ge(y_acc, C)
            sp.dma_start(out.rearrange("(t p) d -> p t d", p=P), base[:, :, :]).then_inc(s_out, 16)
            sp.wait_ge(s_out, 16)

        @block.gpsimd
        def _(pool):
            for m in (ident, ident_h, ident_b, mask_i):
                nc.gpsimd.memset(m[:], 0.0).then_inc(k_set, 1)
            nc.gpsimd.memset(half[:], -0.5).then_inc(k_set, 1)
            nc.gpsimd.memset(xa[:, :, D:D + 1], 1.0).then_inc(k_set, 1)
            nc.gpsimd.iota(rank[:], [[0, SUB], [-1, E_N]], base=E_N, channel_multiplier=0,
                           allow_small_or_imprecise_dtypes=True).then_inc(k_set, 1)
            pool.wait_ge(k_set, 7)
            for m, v in ((ident, 1.0), (ident_h, 1.0), (ident_b, 1.0), (mask_i, MASK)):
                nc.gpsimd.affine_select(out=m[:], in_=m[:], compare_op=ALU.not_equal, fill=v, base=0,
                                        pattern=[[-1, P]], channel_multiplier=1).then_inc(k_id, 1)
            pool.wait_ge(st_ok, 1)
            nc.gpsimd.tensor_tensor(rstd[:], veps[:], half[:], ALU.pow).then_inc(rs_ok, 1)
            with pool.Fori(0, C - 1, 2) as c2:
                for u in range(2):
                    pool.wait_ge(xn_ok, c2 + (u + 1))
                    nc.gpsimd.tensor_copy(xn[:, bass.ds((c2 + u) * SUB, SUB), :], xc[:, u]).then_inc(xn_kept, 1)
                    pool.wait_ge(ss_ok, c2 + (u + 1))
                    nc.gpsimd.tensor_tensor(rn[:, u], ss[:, u], half[:, 0:2 * SUB], ALU.pow).then_inc(rn_ok, 1)
            with pool.Fori(0, C) as c:
                pool.wait_ge(l2_st, c + 1)
                nc.gpsimd.tensor_tensor(rstd[:, 0:SUB], veps[:, 0:SUB], half[:, 0:SUB], ALU.pow).then_inc(l2_rs, 1)

        @block.scalar
        def _(act):
            for dst, src in ((wkq_in[:, 0, :], Wk), (wkq_in[:, 1, :], Wq), (wg[:], Wg),
                             (b1_in[:], b1.rearrange("e (b f) -> (e b) f", f=P)), (b2s[:], b2),
                             (gb[:, 0, :], bg.rearrange("(a e) -> a e", a=1).broadcast_to([P, E_N])),
                             (gb[:, 1, :], bias.rearrange("(a e) -> a e", a=1).broadcast_to([P, E_N]))):
                act.dma_start(dst, src).then_inc(s_w, 16)
            act.dma_start(w1_in[:].rearrange("p (e f) -> p e f", e=E_N), W1.rearrange("e d f -> d e f")).then_inc(s_w1, 16)
            act.dma_start(w2_in.rearrange("p (g d) -> p g d", d=D),
                          W2.rearrange("e (b f) d -> f (e b) d", f=P)).then_inc(s_w1, 16)
            act.wait_ge(wt_ps, 1)
            nc.scalar.activation(wkqh[:], ps_a[:, 0:2 * D], ACT.Copy, scale=W_SCALE).then_inc(wt_h, 1)
            nc.scalar.activation(b1c[:], ps_a[:, 2 * D:2 * D + E_N * FB], ACT.Copy).then_inc(wt_h, 1)
            act.wait_ge(s_w1, 32)
            nc.scalar.activation(w1h[:], w1_in[:], ACT.Copy, scale=W_SCALE).then_inc(wt_h, 1)
            nc.scalar.activation(w2h[:], w2_in, ACT.Copy, scale=W_SCALE).then_inc(wt_h, 1)
            act.wait_ge(wt_l, 2)
            with act.Fori(0, C - 1, 2) as c2:
                for u in range(2):
                    n = c2 + u
                    act.wait_ge(xn_ok, n + 1)
                    nc.scalar.activation(xa[:, bass.ds(n * SUB, SUB), 0:D], xc[:, u], ACT.Copy).then_inc(xh_ok, 1)
                    act.wait_ge(xt_ps, n + 1)
                    nc.scalar.activation(xth[:, u], ps_a[:], ACT.Copy).then_inc(xth_ok, 1)
                    act.wait_ge(kq_ps, n + 1)
                    nc.scalar.activation(kq[:, u], ps_s[:, 0, :], ACT.Copy).then_inc(kq_ok, 1)
                    nc.scalar.activation(sq[:, u], ps_s[:, 0, :], ACT.Square).then_inc(kq_ok, 1)
                    act.wait_ge(kn_ok, n + 1)
                    nc.scalar.activation(kch[:, u].rearrange("p s k d -> p (s k d)"), kq[:, u], ACT.Copy).then_inc(kch_ok, 1)
                    act.wait_ge(kt_ps, n + 1)
                    nc.scalar.activation(kqh[:, :, bass.ds(n * CH, CH)],
                                         ps_s[:, 1, 0:CH].bitcast(F16).rearrange("p (k i) -> p k i", k=2),
                                         ACT.Copy).then_inc(kth_ok, 1)
            with act.Fori(0, C * S - 1, 2) as g2:
                for u in range(2):
                    act.wait_ge(s_ps, g2 + (u + 1))
                    act.wait_ge(el_ok, g2 + (u + 1))
                    nc.scalar.activation(e_f[:, u], ps_s[:, u], ACT.Exp, scale=SC).then_inc(e_ok, 1)
                    act.wait_ge(e_ok, g2 + (u + 1))
                    act.wait_ge(pv, g2 + (u + 1))
                    nc.scalar.activation(e_h[:, u], e_f[:, u], ACT.Copy).then_inc(eh_ok, 1)
            with act.Fori(0, C) as c:
                act.wait_ge(l2_ps, c + 1)
                nc.scalar.activation(xtf[:], ps_a[:], ACT.Copy).then_inc(l2_f, 1)
                nc.scalar.activation(x2h[:, bass.ds(c * CH, CH)], ps_a[:], ACT.Copy).then_inc(l2_h, 1)
                act.wait_ge(g_d, c + 1)
                nc.scalar.activation(gw[:, 1], gw[:, 0], ACT.Exp).then_inc(g_e, 1)
                act.wait_ge(ct_ps, c + 1)
                nc.scalar.activation(ct[:], ps_b[0:E_N, :], ACT.Copy).then_inc(ct_ok, 1)
            with act.Fori(0, C * E_N - 1, 2) as n2:
                for u in range(2):
                    act.wait_ge(z_ps, n2 + (u + 1))
                    act.wait_ge(hl_ok, n2 + (u + 1))
                    for b in range(FB):
                        nc.scalar.activation(e_f[:, u, b * CH:(b + 1) * CH], ps_s[:, u, b * CH:(b + 1) * CH],
                                             ACT.Relu, scale=1.0 / W_SCALE,
                                             bias=b1c[:, bass.ds(((n2 + u) & (E_N - 1)) * FB + b, 1)]).then_inc(h_ok, 1)
                    act.wait_ge(h_ok, (n2 + (u + 1)) * FB)
                    act.wait_ge(y_ps, n2 + (u + 1))
                    nc.scalar.activation(e_h[:, u], e_f[:, u], ACT.Copy).then_inc(hh_ok, 1)

        @block.tensor
        def _(pe):
            pe.wait_ge(k_id, 4)
            pe.wait_ge(s_w, 7 * 16)
            for k in range(2):
                nc.tensor.transpose(ps_a[:, k * D:(k + 1) * D], wkq_in[:, k, :], ident[:])
            nc.tensor.transpose(ps_a[:, 2 * D:2 * D + E_N * FB], b1_in[:],
                                ident[0:E_N * FB, 0:E_N * FB]).then_inc(wt_ps, 1)
            pe.wait_ge(wt_h, 2)
            pe.wait_ge(wt_l, 1)
            with pe.Fori(0, C - 1, 2) as c2:
                for u in range(2):
                    n = c2 + u
                    pe.wait_ge(xn_ok, n + 1)
                    pe.wait_ge(xtl_ok, n)
                    for s in range(SUB):
                        mm = nc.tensor.transpose(ps_a[:, s * P:(s + 1) * P], xc[:, u, s, :], ident[:])
                    mm.then_inc(xt_ps, 1)
                    pe.wait_ge(xth_ok, n + 1)
                    pe.wait_ge(xtl_ok, n + 1)
                    pe.wait_ge(kq_ok, n * 2)
                    for s in range(SUB):
                        o = ps_s[:, 0, s * 2 * D:(s + 1) * 2 * D]
                        t = slice(s * P, (s + 1) * P)
                        nc.tensor.matmul(o, xth[:, u, t], wkqh[:], start=True, stop=False)
                        nc.tensor.matmul(o, xth[:, u, t], wkql[:], start=False, stop=False)
                        mm = nc.tensor.matmul(o, xtl[:, u, t], wkqh[:], start=False, stop=True)
                    mm.then_inc(kq_ps, 1)
                    pe.wait_ge(kch_ok, n + 1)
                    pe.wait_ge(kcl_ok, n + 1)
                    pe.wait_ge(kth_ok, n)
                    pe.wait_ge(ktl_ok, n)
                    for s in range(SUB):
                        for k in range(2):
                            w = slice((k * SUB + s) * P, (k * SUB + s + 1) * P)
                            nc.tensor.transpose(ps_s[:, 1, 0:CH].bitcast(F16)[:, w], kch[:, u, s, k, :], ident_h[:])
                            mm = nc.tensor.transpose(ps_s[:, 1, CH:2 * CH].bitcast(BF16)[:, w], kcl[:, u, s, k, :],
                                                     ident_b[:])
                    mm.then_inc(kt_ps, 1)
            pe.wait_ge(kth_ok, C)
            pe.wait_ge(ktl_ok, C)
            pe.sem_inc(pv, 2)

            def scores(c, p, u):
                n = c * S + p
                pe.wait_ge(conv, n + 1)
                pe.wait_ge(e_ok, n - 1) if not isinstance(n, int) or n > 1 else None
                for b in range(PAIR):
                    o = ps_s[:, u, b * CH:(b + 1) * CH]
                    j = p * SW + b * P
                    ch = bass.ds(c * CH, CH)
                    for s in range(SUB):
                        nc.tensor.matmul(o[:, s * P:(s + 1) * P], noedge[:, s, bass.ds(j, P)], mask_i[:],
                                         start=(s == 0), stop=False, skip_group_check=True)
                    nc.tensor.matmul(o, kqh[:, 1, bass.ds(j, P)], kqh[:, 0, ch], start=False, stop=False,
                                     skip_group_check=True)
                    nc.tensor.matmul(o, kqh[:, 1, bass.ds(j, P)], kql[:, 0, ch], start=False, stop=False,
                                     skip_group_check=True)
                    mm = nc.tensor.matmul(o, kql[:, 1, bass.ds(j, P)], kqh[:, 0, ch], start=False, stop=True,
                                          skip_group_check=True)
                mm.then_inc(s_ps, 1)

            def attend(c, p, u, first=False, last=False):
                n = c * S + p
                pe.wait_ge(el_ok, n + 3)
                if first:
                    pe.wait_ge(o_free, c)
                for b in range(PAIR):
                    j = p * PAIR + b
                    for s in range(SUB):
                        w = slice(b * CH + s * P, b * CH + (s + 1) * P)
                        nc.tensor.matmul(ps_o[:, s, 0:D + 1], e_h[:, u, w], xa[:, bass.ds(j, 1), :].rearrange("p a d -> p (a d)"),
                                         start=(first and b == 0 and s % 2 == 0), stop=False, skip_group_check=True)
                        nc.tensor.matmul(ps_o[:, s, 0:D], e_h[:, u, w], xl[:, bass.ds(j, 1), :].rearrange("p a d -> p (a d)"),
                                         start=False, stop=False, skip_group_check=True)
                        mm = nc.tensor.matmul(ps_o[:, s, 0:D + 1], e_l[:, u, w], xa[:, bass.ds(j, 1), :].rearrange("p a d -> p (a d)"),
                                              start=False, stop=(last and b == 1), skip_group_check=True)
                mm.then_inc(pv, 1)

            def chunk(c):
                scores(c, 0, 0)
                scores(c, 1, 1)
                scores(c, 2, 0)
                attend(c, 0, 0, first=True)
                scores(c, 3, 1)
                attend(c, 1, 1)
                with pe.Fori(2, S - 2 - 1, 2) as p2:
                    for u in range(2):
                        scores(c, p2 + (u + 2), u)
                        attend(c, p2 + u, u)
                attend(c, S - 2, 0)
                attend(c, S - 1, 1, last=True)

            chunk(0)
            with pe.Fori(1, C) as c:
                chunk(c)

            with pe.Fori(0, C) as c:
                pe.wait_ge(l2_x, c + 1)
                pe.wait_ge(l2_l, c)
                for s in range(SUB):
                    mm = nc.tensor.transpose(ps_a[:, s * P:(s + 1) * P], xc[:, 0, s, :], ident[:])
                mm.then_inc(l2_ps, 1)
                pe.wait_ge(l2_f, c + 1)
                pe.wait_ge(c_ok, c)
                for s in range(SUB):
                    mm = nc.tensor.matmul(ps_o[:, 0, s * E_N:(s + 1) * E_N], xtf[:, s * P:(s + 1) * P], wg[:],
                                          start=True, stop=True)
                mm.then_inc(g_ps, 1)
                pe.wait_ge(c_ok, c + 1)
                for s in range(SUB):
                    mm = nc.tensor.transpose(ps_b[0:E_N, s * P:(s + 1) * P], cfull[:, s, :], ident[:])
                mm.then_inc(ct_ps, 1)
                pe.wait_ge(ct_ok, c + 1)
                for s in range(SUB):
                    mm = nc.tensor.matmul(ps_o[:, 2 + s // 2, (s % 2) * P:(s % 2 + 1) * P], ct[:, s * P:(s + 1) * P],
                                          b2s[:], start=True, stop=True)
                mm.then_inc(b2_ps, 1)
            pe.wait_ge(b2_ok, C)
            pe.sem_inc(y_ps, 2)

            def hidden(c, e, u):
                n = c * E_N + e
                if not isinstance(n, int) or n > 1:
                    pe.wait_ge(h_ok, (n - 1) * FB)
                ch = bass.ds(c * CH, CH)
                for b in range(FB):
                    o = ps_s[:, u, b * CH:(b + 1) * CH]
                    f = bass.ds(e * F + b * P, P)
                    nc.tensor.matmul(o, w1h[:, f], x2h[:, ch], start=True, stop=False)
                    nc.tensor.matmul(o, w1h[:, f], x2l[:, ch], start=False, stop=False)
                    mm = nc.tensor.matmul(o, w1l[:, f], x2h[:, ch], start=False, stop=True)
                mm.then_inc(z_ps, 1)

            def project(c, e, u):
                n = c * E_N + e
                pe.wait_ge(hl_ok, n + 3)
                pe.wait_ge(y_ok, n + 1)
                for s in range(SUB):
                    o = ps_o[:, 2 * u + s // 2, (s % 2) * P:(s % 2 + 1) * P]
                    for b in range(FB):
                        w = slice(b * CH + s * P, b * CH + (s + 1) * P)
                        d = bass.ds((e * FB + b) * D, D)
                        nc.tensor.matmul(o, e_h[:, u, w], w2h[:, d], start=(b == 0), stop=False)
                        nc.tensor.matmul(o, e_h[:, u, w], w2l[:, d], start=False, stop=False)
                        mm = nc.tensor.matmul(o, e_l[:, u, w], w2h[:, d], start=False, stop=(b == FB - 1))
                mm.then_inc(y_ps, 1)

            def experts(c):
                hidden(c, 0, 0)
                hidden(c, 1, 1)
                with pe.Fori(0, E_N - 2 - 1, 2) as e2:
                    for u in range(2):
                        hidden(c, e2 + (u + 2), u)
                        project(c, e2 + u, u)
                project(c, E_N - 2, 0)
                project(c, E_N - 1, 1)
            experts(0)
            with pe.Fori(1, C) as c:
                experts(c)

        @block.vector
        def _(dve):
            V = nc.vector
            dve.wait_ge(wt_h, 2)
            V.scalar_tensor_tensor(wkql[:], ps_a[:, 0:2 * D], W_SCALE, wkqh[:], ALU.mult, ALU.subtract).then_inc(wt_l, 1)
            dve.wait_ge(s_x, 16)
            for t in range(T):
                V.bn_stats(st[:, t, :], base[:, t, :])
            dve.drain()
            for t in range(T):
                V.bn_aggr(mv[:, t, :], st[:, t, :])
            dve.drain()
            V.tensor_scalar(veps[:], mv[:, :, 1], LN_EPS, None, ALU.add).then_inc(st_ok, 1)
            dve.wait_ge(wt_h, 4)
            V.scalar_tensor_tensor(w1l[:], w1_in[:], W_SCALE, w1h[:], ALU.mult, ALU.subtract).then_inc(wt_l, 1)
            V.scalar_tensor_tensor(w2l[:], w2_in, W_SCALE, w2h[:], ALU.mult, ALU.subtract)
            dve.wait_ge(rs_ok, 1)
            with dve.Fori(0, C - 1, 2) as c2:
                for u in range(2):
                    n = c2 + u
                    dve.wait_ge(xn_kept, n)
                    for s in range(SUB):
                        V.tensor_scalar(xc[:, u, s, :], base[:, bass.ds(n * SUB + s, 1), :].rearrange("p a d -> p (a d)"),
                                        mv[:, bass.ds(n * SUB + s, 1), 0], rstd[:, bass.ds(n * SUB + s, 1)],
                                        ALU.subtract, ALU.mult)
                    dve.drain().then_inc(xn_ok, 1)
                    bt = base[:, bass.ds(n * SUB, SUB), :]
                    V.scalar_tensor_tensor(bt, xc[:, u], 0.5, bt, ALU.mult, ALU.add)
                    dve.wait_ge(xh_ok, n + 1)
                    V.tensor_tensor(xl[:, bass.ds(n * SUB, SUB), :], xc[:, u], xa[:, bass.ds(n * SUB, SUB), 0:D], ALU.subtract)
                    dve.wait_ge(xth_ok, n + 1)
                    V.tensor_tensor(xtl[:, u], ps_a[:], xth[:, u], ALU.subtract).then_inc(xtl_ok, 1)
                    dve.wait_ge(kq_ok, (n + 1) * 2)
                    V.tensor_reduce(ss[:, u], sq[:, u].rearrange("p (a d) -> p a d", d=D), AX_X, ALU.add)
                    dve.drain()
                    V.tensor_scalar(ss[:, u], ss[:, u], (W_SCALE * COS_EPS) ** 2, None, ALU.max).then_inc(ss_ok, 1)
                    dve.wait_ge(rn_ok, n + 1)
                    k3 = kq[:, u].rearrange("p (a d) -> p a d", d=D)
                    V.scalar_tensor_tensor(k3, k3, UNIT_SCALE, rn[:, u].unsqueeze(2).broadcast_to([P, 2 * SUB, D]),
                                           ALU.mult, ALU.mult).then_inc(kn_ok, 1)
                    dve.wait_ge(kch_ok, n + 1)
                    V.tensor_tensor(kcl[:, u].rearrange("p s k d -> p (s k d)"), kq[:, u],
                                    kch[:, u].rearrange("p s k d -> p (s k d)"), ALU.subtract).then_inc(kcl_ok, 1)
                    dve.wait_ge(kt_ps, n + 1)
                    V.tensor_copy(kql[:, :, bass.ds(n * CH, CH)],
                                  ps_s[:, 1, CH:2 * CH].bitcast(BF16).rearrange("p (k i) -> p k i", k=2)
                                  ).then_inc(ktl_ok, 1)

            def convert(p, b, q):
                V.tensor_scalar(noedge[:, :, bass.ds(p * SW, SW)], adj_in[:, b, :, q * SW:(q + 1) * SW],
                                0, None, ALU.is_le).then_inc(conv, 1)

            dve.sem_inc(el_ok, 2)
            for p in range(S):
                if p % QS == 0:
                    dve.wait_ge(s_adj[p // QS % 2], 16 * (p // QS // 2 + 1))
                convert(p, p // QS % 2, p % QS)

            def low(n, u):
                dve.wait_ge(eh_ok, n + 1)
                dve.wait_ge(pv, n + 1)
                V.tensor_tensor(e_l[:, u], e_f[:, u], e_h[:, u], ALU.subtract).then_inc(el_ok, 1)

            def finish(c):
                dve.wait_ge(pv, (c + 1) * S + 2)
                V.tensor_scalar(den[:], ps_o[:, :, D], TINY, None, ALU.max)
                V.tensor_scalar(alone[:], ps_o[:, :, D], 0.0, 0.5, ALU.is_le, ALU.mult)
                dve.drain()
                V.reciprocal(rden[:], den[:])
                dve.drain()
                V.scalar_tensor_tensor(mx_t[:], ps_o[:, :, 0:D], 0.5, rden[:].unsqueeze(2).broadcast_to([P, SUB, D]),
                                       ALU.mult, ALU.mult).then_inc(o_free, 1)
                bt = base[:, bass.ds(c * SUB, SUB), :]
                dve.drain()
                V.tensor_tensor(bt, bt, mx_t[:], ALU.add)
                dve.drain()
                V.tensor_tensor(mx_t[:], xn[:, bass.ds(c * SUB, SUB), :], alone[:].unsqueeze(2).broadcast_to([P, SUB, D]),
                                ALU.mult)
                dve.drain()
                V.tensor_tensor(bt, bt, mx_t[:], ALU.add)
                dve.drain()

            with dve.Fori(0, C - 1) as c:
                with dve.Fori(0, NQ - 1, 2) as q2:
                    for b in range(2):
                        for q in range(QS):
                            p = (q2 + b) * QS + q
                            low(c * S + p, q % 2)
                            if q == 0:
                                dve.wait_ge(s_adj[b], ((c + 1) * (NQ // 2) + (q2 >> 1) + 1) * 16)
                            convert(p, b, q)
                finish(c)
            with dve.Fori(0, S - 1, 2) as p2:
                for u in range(2):
                    low((C - 1) * S + p2 + u, u)
            finish(C - 1)

            with dve.Fori(0, C) as c:
                bt = base[:, bass.ds(c * SUB, SUB), :]
                for s in range(SUB):
                    V.bn_stats(st[:, s, :], base[:, bass.ds(c * SUB + s, 1), :].rearrange("p a d -> p (a d)"))
                dve.drain()
                for s in range(SUB):
                    V.bn_aggr(mv[:, s, :], st[:, s, :])
                dve.drain()
                V.tensor_scalar(veps[:, 0:SUB], mv[:, 0:SUB, 1], LN_EPS, None, ALU.add).then_inc(l2_st, 1)
                dve.wait_ge(l2_rs, c + 1)
                for s in range(SUB):
                    V.tensor_scalar(xc[:, 0, s, :], base[:, bass.ds(c * SUB + s, 1), :].rearrange("p a d -> p (a d)"),
                                    mv[:, s, 0:1], rstd[:, s:s + 1], ALU.subtract, ALU.mult)
                dve.drain().then_inc(l2_x, 1)
                dve.wait_ge(l2_h, c + 1)
                V.tensor_tensor(x2l[:, bass.ds(c * CH, CH)], ps_a[:], x2h[:, bass.ds(c * CH, CH)], ALU.subtract).then_inc(l2_l, 1)
                dve.wait_ge(g_ps, c + 1)
                V.tensor_tensor(lg[:], ps_o[:, 0, 0:SUB * E_N].rearrange("p (s e) -> p s e", e=E_N),
                                gb[:, 0:1, :].broadcast_to([P, SUB, E_N]), ALU.add)
                dve.drain()
                V.tensor_tensor(lg[:], lg[:], gb[:, 1:2, :].broadcast_to([P, SUB, E_N]), ALU.add)
                dve.drain()

                def pick(lgt, v, r, oh):
                    V.tensor_reduce(top[:, v], lgt[:], AX_X, ALU.max)
                    dve.drain()
                    V.tensor_tensor(cand[:], lgt[:], top[:, v].unsqueeze(2).broadcast_to([P, SUB, E_N]), ALU.is_equal)
                    dve.drain()
                    V.tensor_tensor(cand[:], cand[:], rank[:], ALU.mult)
                    dve.drain()
                    V.tensor_reduce(top[:, r], cand[:], AX_X, ALU.max)
                    dve.drain()
                    V.tensor_tensor(oh[:], rank[:], top[:, r].unsqueeze(2).broadcast_to([P, SUB, E_N]), ALU.is_equal)
                    dve.drain()

                pick(lg, 0, 2, oh1)
                V.tensor_reduce(top[:, 1], lg[:], AX_X, ALU.min)
                dve.drain()
                V.tensor_tensor(gw[:, 0], top[:, 0], top[:, 1], ALU.subtract)
                dve.drain()
                V.tensor_scalar(gw[:, 0], gw[:, 0], 2.0, 1.0, ALU.mult, ALU.add)
                dve.drain()
                V.tensor_tensor(lg2[:], oh1[:], gw[:, 0].unsqueeze(2).broadcast_to([P, SUB, E_N]), ALU.mult)
                dve.drain()
                V.tensor_tensor(lg2[:], lg[:], lg2[:], ALU.subtract)
                dve.drain()
                pick(lg2, 1, 3, oh2)
                V.tensor_tensor(gw[:, 0], top[:, 1], top[:, 0], ALU.subtract).then_inc(g_d, 1)
                dve.wait_ge(g_e, c + 1)
                V.tensor_scalar(gw[:, 2], gw[:, 1], 1.0, None, ALU.add)
                dve.drain()
                V.reciprocal(gw[:, 2], gw[:, 2])
                dve.drain()
                V.tensor_tensor(gw[:, 3], gw[:, 1], gw[:, 2], ALU.mult)
                V.tensor_tensor(oh1[:], oh1[:], gw[:, 2].unsqueeze(2).broadcast_to([P, SUB, E_N]), ALU.mult)
                dve.drain()
                V.tensor_tensor(oh2[:], oh2[:], gw[:, 3].unsqueeze(2).broadcast_to([P, SUB, E_N]), ALU.mult)
                dve.drain()
                V.tensor_tensor(cfull[:], oh1[:], oh2[:], ALU.add).then_inc(c_ok, 1)
                dve.drain()
                V.tensor_scalar(cw[:, bass.ds(c * SUB, SUB), :], cfull[:], 1.0 / W_SCALE, None, ALU.mult)
                dve.wait_ge(b2_ps, c + 1)
                V.tensor_tensor(bt, bt, ps_o[:, 2:4, :].rearrange("p a (b d) -> p (a b) d", d=D), ALU.add).then_inc(b2_ok, 1)
                dve.drain()

            dve.sem_inc(hl_ok, 2)
            dve.sem_inc(y_ok, 2)

            def low_h(n, u):
                dve.wait_ge(hh_ok, n + 1)
                dve.wait_ge(y_ps, n + 1)
                V.tensor_tensor(e_l[:, u], e_f[:, u], e_h[:, u], ALU.subtract).then_inc(hl_ok, 1)

            def gather(c, n, e, u):
                dve.wait_ge(y_ps, n + 3)
                y = ps_o[:, 2 * u:2 * u + 2, :].rearrange("p a (b d) -> p (a b) d", d=D)
                V.tensor_tensor(mx_t[:], y, cw[:, bass.ds(c * SUB, SUB), bass.ds(e, 1)].broadcast_to([P, SUB, D]),
                                ALU.mult).then_inc(y_ok, 1)
                bt = base[:, bass.ds(c * SUB, SUB), :]
                dve.drain()
                V.tensor_tensor(bt, bt, mx_t[:], ALU.add)
                dve.drain()

            with dve.Fori(0, C) as c:
                low_h(c * E_N, 0)
                with dve.Fori(0, E_N - 2 - 1, 2) as e2:
                    low_h(c * E_N + e2 + 1, 1)
                    gather(c, c * E_N + e2, e2, 0)
                    low_h(c * E_N + e2 + 2, 0)
                    gather(c, c * E_N + e2 + 1, e2 + 1, 1)
                low_h(c * E_N + E_N - 1, 1)
                gather(c, c * E_N + E_N - 2, E_N - 2, 0)
                gather(c, c * E_N + E_N - 1, E_N - 1, 1)
                dve.drain().then_inc(y_acc, 1)


_INS = ["x", "adj", "L0_gnn_Wq", "L0_gnn_Wk", "L0_ffn_Wg", "L0_ffn_bg", "L0_ffn_bias",
        "L0_ffn_W1", "L0_ffn_b1", "L0_ffn_W2", "L0_ffn_b2"]
_OUTS = [((4096, 128), "float32")]


def kernel(**inputs):
    import numpy as _np
    import concourse.bacc as _bacc
    from concourse import mybir as _mybir
    from concourse.bass_utils import run_bass_kernel_spmd as _run

    nc = _bacc.Bacc("TRN2", target_bir_lowering=False, num_devices=1)
    arrays, args = {}, []
    for name in _INS:
        a = _np.ascontiguousarray(inputs[name])
        arrays[f"in_{name}_dram"] = a
        args.append(nc.dram_tensor(f"in_{name}_dram", a.shape, _mybir.dt.from_np(a.dtype), kind="ExternalInput").ap())
    for i, (shape, dtype) in enumerate(_OUTS):
        dt = _mybir.dt.from_np(_np.dtype(dtype))
        args.append(nc.dram_tensor(f"out_{i}_dram", shape, dt, kind="ExternalOutput").ap())
    gnn_moe_layer(nc, *args)
    r = _run(nc, [arrays], core_ids=[0])
    got = tuple(r.results[0][f"out_{i}_dram"] for i in range(len(_OUTS)))
    return got[0]
```

```python
from contextlib import ExitStack

import concourse.bass as bass
from concourse import mybir

F32 = mybir.dt.float32
F16 = mybir.dt.float16
BF16 = mybir.dt.bfloat16
I32 = mybir.dt.int32
ALU = mybir.AluOpType
ACT = mybir.ActivationFunctionType
AX_X = mybir.AxisListType.X

P = 128
SUB = 4
PAIR = 2
AHEAD = 4
RING = 8
LN_EPS = 1e-5
COS_EPS = 1e-4
W_SCALE = 64.0
UNIT_SCALE = 256.0
MASK = -float(2 ** 30)
TINY = 1e-30
LEAST = 1.2e-38


def gnn_moe_layer(nc, x, adj, Wq, Wk, Wg, bg, bias, W1, b1, W2, b2, out):
    N, D = x.shape
    E_N, _, F = W1.shape
    T = N // P
    CH = SUB * P
    C = N // CH
    SW = PAIR * P
    S = N // SW
    QS = 4
    QW = QS * SW
    NQ = N // QW
    FB = F // P
    B = E_N * FB
    LAG = 2
    MID, LATE = S // 2, 3 * S // 4
    PREP = 4
    SC = 1.0 / (UNIT_SCALE * UNIT_SCALE)
    assert B == S and D == P and FB == PAIR

    with ExitStack() as ctx:
        def sb(name, shape, dt):
            return ctx.enter_context(nc.sbuf_tensor(name, shape, dt))

        def ps(name, shape, dt):
            return ctx.enter_context(nc.psum_tensor(name, shape, dt))

        def sem(name):
            return ctx.enter_context(nc.semaphore(name))

        base = sb("base", [P, T, D], F32)
        xn = sb("xn", [P, T, D], F32)
        xa = sb("xa", [P, T, D + 1], F16)
        xl = sb("xl", [P, T, D], BF16)
        kqh = sb("kqh", [P, 2, N], F16)
        kql = sb("kql", [P, 2, N], BF16)
        adj_in = sb("adj_in", [P, 2, SUB, QW], I32)
        noedge = sb("noedge", [P, RING, SUB, SW], BF16)
        e_f = sb("e_f", [P, 2, PAIR * CH], F32)
        e_h = sb("e_h", [P, 2, PAIR * CH], F16)
        e_l = sb("e_l", [P, 2, PAIR * CH], BF16)
        w1h = sb("w1h", [P, E_N * F], F16)
        w1l = sb("w1l", [P, E_N * F], BF16)
        w2h = sb("w2h", [P, B * D], F16)
        w2l = sb("w2l", [P, B * D], BF16)
        w1_in = sb("w1_in", [P, E_N * F], F32)
        w2_in = adj_in[:, 1, 0:2, :].bitcast(F32).rearrange("p s n -> p (s n)")
        wkq_in = sb("wkq_in", [P, 2, D], F32)
        wkqh = sb("wkqh", [P, 2 * D], F16)
        wkql = sb("wkql", [P, 2 * D], BF16)
        wg = sb("wg", [P, E_N], F32)
        gb = sb("gb", [P, 2, E_N], F32)
        b1_in = sb("b1_in", [B, P], F32)
        b1c = sb("b1c", [P, B], F32)
        b2_in = sb("b2_in", [1, 3, E_N * D], F32)
        b2_s = sb("b2_s", [1, 3, E_N * D], BF16)
        b2_p = sb("b2_p", [3, E_N * D], BF16)
        ones3 = sb("ones3", [3, P], BF16)
        zero1 = sb("zero1", [1, 2 * D], F16)
        ident = sb("ident", [P, P], F32)
        ident_h = sb("ident_h", [P, P], F16)
        ident_b = sb("ident_b", [P, P], BF16)
        mask_i = sb("mask_i", [P, P], BF16)
        half = sb("half", [P, T], F32)
        least = sb("least", [P, E_N, E_N], F32)
        st = sb("st", [P, T, 6], F32)
        mv = sb("mv", [P, T, 2], F32)
        veps = sb("veps", [P, T], F32)
        rstd = sb("rstd", [P, T], F32)
        xc = sb("xc", [P, 2, SUB, D], F32)
        xth = sb("xth", [P, 2, CH], F16)
        xtl = sb("xtl", [P, 2, CH], BF16)
        ss = sb("ss", [P, 2, SUB * 2], F32)
        rn = sb("rn", [P, 2, SUB * 2], F32)
        den = sb("den", [P, 2, SUB], F32)
        self_w = sb("self_w", [P, SUB], F32)
        lg = sb("lg", [P, SUB, E_N], F32)
        diff = sb("diff", [P, SUB, E_N, E_N], F32)
        rank = sb("rank", [P, SUB, E_N], F32)
        top = sb("top", [P, 2, SUB], F32)
        pe_ = sb("gate_e", [P, SUB, E_N], F32)
        cw = sb("cw", [P, 2, SUB, E_N], F32)
        xtf = sb("xtf", [P, CH], F32)
        kn, kch, kcl = e_f, e_h, e_l
        sq = noedge[:, AHEAD:].rearrange("p (u r) s j -> p u (r s j)", u=2).bitcast(F32)
        h_f = w1_in[:, 0:2 * CH].rearrange("p (u n) -> p u n", u=2)
        h_h = w1_in[:, 2 * CH:3 * CH].bitcast(F16).rearrange("p (u n) -> p u n", u=2)
        h_l = w1_in[:, 3 * CH:4 * CH].bitcast(BF16).rearrange("p (u n) -> p u n", u=2)
        x2h, x2l = kqh[:, 0, :], kql[:, 0, :]

        ps_s = ps("ps_s", [P, 2, PAIR * CH], F32)
        ps_o = ps("ps_o", [P, SUB, 2 * P], F32)
        ps_z = ps("ps_z", [P, CH], F32)
        ps_y = ps("ps_y", [P, SUB, D], F32)
        kq_rows = [ps_s[:, 0, :], ps_o[:].rearrange("p s d -> p (s d)")]
        y_of = [ps_y[:], ps_o[:, 0:2, :].rearrange("p s (h d) -> p (s h) d", d=D)]

        x_in = [sem(f"x_in{i}") for i in range(4)]
        w_in = sem("w_in")
        wff_in = sem("wff_in")
        adj_s = [sem("adj_in0"), sem("adj_in1")]
        b2_moved = sem("b2_moved")
        out_s = sem("out_s")
        k_set = sem("k_set")
        k_ok = sem("k_ok")
        wt_ps = sem("wt_ps")
        w_h = sem("w_h")
        w_l = sem("w_l")
        b2_ok = sem("b2_ok")
        st_ok = sem("st_ok")
        rs_ok = sem("rs_ok")
        xc_ok = sem("xc_ok")
        xa_ok = sem("xa_ok")
        xn_ok = sem("xn_ok")
        xl_ok = sem("xl_ok")
        xt_ps = sem("xt_ps")
        xth_ok = sem("xth_ok")
        xtl_ok = sem("xtl_ok")
        kq_ps = sem("kq_ps")
        sq_ok = sem("sq_ok")
        ss_ok = sem("ss_ok")
        rn_ok = sem("rn_ok")
        kn_ok = sem("kn_ok")
        kch_ok = sem("kch_ok")
        kcl_ok = sem("kcl_ok")
        kt_ps = sem("kt_ps")
        kth_ok = sem("kth_ok")
        ktl_ok = sem("ktl_ok")
        conv = sem("conv")
        s_ps = sem("s_ps")
        e_ok = sem("e_ok")
        eh_ok = sem("eh_ok")
        el_ok = sem("el_ok")
        pv = sem("pv")
        o_free = sem("o_free")
        l2_st = sem("l2_st")
        l2_rs = sem("l2_rs")
        l2_x = sem("l2_x")
        t_ps = sem("t_ps")
        t_f = sem("t_f")
        t_h = sem("t_h")
        t_l = sem("t_l")
        g_ps = sem("g_ps")
        g_rd = sem("g_rd")
        g_d = sem("g_d")
        g_e = sem("g_e")
        z_ps = sem("z_ps")
        h_ok = sem("h_ok")
        hh_ok = sem("hh_ok")
        hl_ok = sem("hl_ok")
        y_ps = sem("y_ps")
        done = sem("done")

        block = ctx.enter_context(nc.Block())

        def tile(m, t):
            return m[:, bass.ds(t, 1), :].rearrange("p a d -> p (a d)")

        def exists(n):
            return not isinstance(n, int) or 0 <= n < C

        def turns(eng, lo, turn):
            for n in range(lo, 1):
                turn(n, n % 2)
            with eng.Fori(1, C - 4, 2) as n1:
                for k in range(2):
                    turn(n1 + k, 1 - k)
            for n in range(C - 3, C + 1):
                turn(n, n % 2)

        def chunk_loops(eng, chunk):
            chunk(0, False, False)
            chunk(1, False, False)
            with eng.Fori(LAG, C - 1) as c:
                chunk(c, True, False)
            chunk(C - 1, True, True)

        @block.sync
        def _(sp):
            for i in range(4):
                n = T // 4
                sp.dma_start(base[:, i * n:(i + 1) * n, :],
                             x.rearrange("(i t p) d -> i p t d", i=4, p=P)[i]).then_inc(x_in[i], 16)
            rows = adj.rearrange("(c s p) (q w) -> c q p s w", s=SUB, p=P, w=QW)

            def load_adj(c, q):
                sp.dma_start(adj_in[:, q % 2], rows[c, q]).then_inc(adj_s[q % 2], 16)
            sp.wait_ge(w_l, 3)
            for q in range(NQ):
                if q >= 2:
                    sp.wait_ge(conv, QS * (q - 1))
                load_adj(0, q)
            with sp.Fori(1, C) as c:
                for q in range(NQ):
                    sp.wait_ge(conv, c * S + QS * (q - 1))
                    load_adj(c, q)
            with sp.Fori(0, C) as c:
                sp.wait_ge(done, c + 1)
                sp.dma_start(out.rearrange("(c s p) d -> c p s d", s=SUB, p=P)[c],
                             base[:, bass.ds(c * SUB, SUB), :]).then_inc(out_s, 16)
            sp.wait_ge(out_s, 16 * C)

        @block.gpsimd
        def _(pool):
            for m, v in ((ident, 0.0), (ident_h, 0.0), (ident_b, 0.0), (mask_i, 0.0), (half, -0.5),
                         (least, LEAST), (ones3, 1.0), (zero1, 0.0)):
                nc.gpsimd.memset(m[:], v).then_inc(k_set, 1)
            nc.gpsimd.memset(xa[:, :, D:D + 1], 1.0).then_inc(k_set, 1)
            pool.wait_ge(k_set, 9)
            for m, v in ((ident, 1.0), (ident_h, 1.0), (ident_b, 1.0), (mask_i, MASK)):
                nc.gpsimd.affine_select(out=m[:], in_=m[:], compare_op=ALU.not_equal, fill=v, base=0,
                                        pattern=[[-1, P]], channel_multiplier=1).then_inc(k_ok, 1)
            nc.gpsimd.affine_select(out=least[:], in_=least[:], compare_op=ALU.is_ge, fill=0.0, base=0,
                                    pattern=[[-1, E_N], [1, E_N]], channel_multiplier=0).then_inc(k_ok, 1)
            for i in range(4):
                pool.wait_ge(st_ok, i + 1)
                r = slice(i * T // 4, (i + 1) * T // 4)
                nc.gpsimd.tensor_tensor(rstd[:, r], veps[:, r], half[:, r], ALU.pow).then_inc(rs_ok, 1)

            def turn(n, u):
                if exists(n + 2):
                    pool.wait_ge(xa_ok, n + 3)
                    t = bass.ds((n + 2) * SUB, SUB)
                    nc.gpsimd.tensor_tensor(xl[:, t, :], xc[:, u], xa[:, t, 0:D], ALU.subtract).then_inc(xl_ok, 1)
                if exists(n + 1):
                    pool.wait_ge(ss_ok, n + 2)
                    nc.gpsimd.tensor_tensor(rn[:, 1 - u], ss[:, 1 - u], half[:, 0:2 * SUB], ALU.pow).then_inc(rn_ok, 1)
            turns(pool, -2, turn)
            with pool.Fori(0, C) as c:
                pool.wait_ge(l2_st, c + 1)
                nc.gpsimd.tensor_tensor(rstd[:, 0:SUB], veps[:, 0:SUB], half[:, 0:SUB], ALU.pow).then_inc(l2_rs, 1)

        @block.scalar
        def _(act):
            A = nc.scalar
            for dst, src in ((wkq_in[:, 0, :], Wk), (wkq_in[:, 1, :], Wq),
                             (b1_in[:], b1.rearrange("e (b f) -> (e b) f", f=P)), (wg[:], Wg),
                             (b2_in[:, 0, :], b2.rearrange("(a e) d -> a (e d)", a=1)),
                             (gb[:, 0, :], bg.rearrange("(a e) -> a e", a=1).broadcast_to([P, E_N])),
                             (gb[:, 1, :], bias.rearrange("(a e) -> a e", a=1).broadcast_to([P, E_N]))):
                act.dma_start(dst, src).then_inc(w_in, 16)
            act.dma_start(w1_in[:].rearrange("p (e f) -> p e f", e=E_N),
                          W1.rearrange("e d f -> d e f")).then_inc(wff_in, 16)
            act.dma_start(w2_in.rearrange("p (g d) -> p g d", d=D),
                          W2.rearrange("e (b f) d -> f (e b) d", f=P)).then_inc(wff_in, 16)
            act.wait_ge(wt_ps, 1)
            A.activation(wkqh[:], ps_y[:, 0:2, :].rearrange("p a d -> p (a d)"), ACT.Copy, scale=W_SCALE).then_inc(w_h, 1)
            A.activation(b1c[:], ps_y[:, 2, 0:B], ACT.Copy).then_inc(w_h, 1)

            def turn(n, u):
                if exists(n - 1):
                    act.wait_ge(kt_ps, n)
                    A.activation(kqh[:, :, bass.ds((n - 1) * CH, CH)],
                                 ps_s[:, 1, 0:CH].bitcast(F16).rearrange("p (k i) -> p k i", k=2),
                                 ACT.Copy).then_inc(kth_ok, 1)
                if exists(n):
                    act.wait_ge(kn_ok, n + 1)
                    A.activation(kch[:, u], kn[:, u], ACT.Copy).then_inc(kch_ok, 1)
                if exists(n + 1):
                    act.wait_ge(kq_ps, n + 2)
                    A.activation(sq[:, 1 - u], kq_rows[1 - u], ACT.Square).then_inc(sq_ok, 1)
                if exists(n + 2):
                    t = bass.ds((n + 2) * SUB, SUB)
                    act.wait_ge(xc_ok, n + 3)
                    A.activation(xa[:, t, 0:D], xc[:, u], ACT.Copy).then_inc(xa_ok, 1)
                    act.wait_ge(xt_ps, n + 3)
                    A.activation(xth[:, u], ps_z[:], ACT.Copy).then_inc(xth_ok, 1)
                    A.activation(xn[:, t, :], xc[:, u], ACT.Copy).then_inc(xn_ok, 1)
            turn(-2, 0)
            turn(-1, 1)
            act.wait_ge(wff_in, 32)
            A.activation(w2h[:], w2_in, ACT.Copy, scale=W_SCALE).then_inc(w_h, 1)
            A.activation(w1h[:], w1_in[:], ACT.Copy, scale=W_SCALE).then_inc(w_h, 1)
            turns(act, 0, turn)

            def exps(n, u):
                act.wait_ge(s_ps, n + 1)
                A.activation(e_f[:, u], ps_s[:, u], ACT.Exp, scale=SC).then_inc(e_ok, 1)
                act.wait_ge(e_ok, n + 1)
                A.activation(e_h[:, u], e_f[:, u], ACT.Copy).then_inc(eh_ok, 1)

            def hidden(m, p, u, src, others=False):
                act.wait_ge(z_ps, m + 1)
                if others:
                    act.wait_ge(hl_ok, m - 1)
                A.activation(h_f[:, u], src, ACT.Relu, scale=1.0 / W_SCALE, bias=b1c[:, bass.ds(p, 1)]).then_inc(h_ok, 1)
                act.wait_ge(h_ok, m + 1)
                if others:
                    act.wait_ge(y_ps, m - 1)
                A.activation(h_h[:, u], h_f[:, u], ACT.Copy).then_inc(hh_ok, 1)

            def transposed(c):
                act.wait_ge(t_ps, c + 1)
                A.activation(xtf[:], ps_z[:], ACT.Copy).then_inc(t_f, 1)
                A.activation(x2h[:, bass.ds(c * CH, CH)], ps_z[:], ACT.Copy).then_inc(t_h, 1)

            def gate(c):
                act.wait_ge(g_d, c + 1)
                A.activation(pe_[:], lg[:], ACT.Exp).then_inc(g_e, 1)

            exps(0, 0)

            def chunk(c, ffn, last):
                prep = not isinstance(c, int) or c > 0
                for p in range(S):
                    u, n = p % 2, c * S + p
                    if ffn:
                        hidden((c - LAG) * B + p, p, u, ps_z[:])
                    if prep and p == MID - 1:
                        transposed(c - 1)
                    if not (last and p == S - 1):
                        if prep or p > 0:
                            act.wait_ge(el_ok, n)
                            act.wait_ge(pv, n)
                        exps(n + 1, 1 - u)
                    if prep and p == LATE:
                        gate(c - 1)
                    if not ffn and c == 0 and p == LATE:
                        act.wait_ge(b2_ok, 5)
                        for i in range(3):
                            act.dma_start(b2_p[i:i + 1, :], b2_s[:, i, :]).then_inc(b2_moved, 16)
            chunk_loops(act, chunk)

            def experts(c, lo, hi):
                with act.Fori(lo, hi - 1, 2) as e0:
                    for v in range(2):
                        for u in range(FB):
                            p = (e0 + v) * FB + u
                            hidden(c * B + p, p, u, ps_s[:, v, u * CH:(u + 1) * CH], others=True)
            experts(C - 2, 0, PREP + 2)
            transposed(C - 1)
            experts(C - 2, PREP + 2, PREP + 4)
            gate(C - 1)
            if PREP + 4 < E_N:
                experts(C - 2, PREP + 4, E_N)
            experts(C - 1, 0, E_N)

        @block.tensor
        def _(pe):
            M = nc.tensor
            pe.wait_ge(k_ok, 5)
            pe.wait_ge(w_in, 7 * 16)
            for k in range(2):
                M.transpose(ps_y[:, k, :], wkq_in[:, k, :], ident[:])
            M.transpose(ps_y[:, 2, 0:B], b1_in[:], ident[0:B, 0:B]).then_inc(wt_ps, 1)

            def turn(n, u):
                if exists(n + 1):
                    pe.wait_ge(xth_ok, n + 2)
                    pe.wait_ge(xtl_ok, n + 2)
                    for s in range(SUB):
                        o = kq_rows[1 - u][:, s * 2 * D:(s + 1) * 2 * D]
                        t = slice(s * P, (s + 1) * P)
                        M.matmul(o, xth[:, 1 - u, t], wkqh[:], start=True, stop=False)
                        M.matmul(o, xth[:, 1 - u, t], wkql[:], start=False, stop=False)
                        mm = M.matmul(o, xtl[:, 1 - u, t], wkqh[:], start=False, stop=True)
                    mm.then_inc(kq_ps, 1)
                if exists(n + 2):
                    pe.wait_ge(xc_ok, n + 3)
                    for s in range(SUB):
                        mm = M.transpose(ps_z[:, s * P:(s + 1) * P], xc[:, u, s, :], ident[:])
                    mm.then_inc(xt_ps, 1)
                if exists(n):
                    pe.wait_ge(kch_ok, n + 1)
                    pe.wait_ge(kcl_ok, n + 1)
                    for s in range(SUB):
                        for k in range(2):
                            i = slice((2 * s + k) * D, (2 * s + k + 1) * D)
                            w = slice((k * SUB + s) * P, (k * SUB + s + 1) * P)
                            M.transpose(ps_s[:, 1, 0:CH].bitcast(F16)[:, w], kch[:, u, i], ident_h[:])
                            mm = M.transpose(ps_s[:, 1, CH:2 * CH].bitcast(BF16)[:, w], kcl[:, u, i], ident_b[:])
                    mm.then_inc(kt_ps, 1)

            turn(-2, 0)
            pe.wait_ge(w_h, 1)
            pe.wait_ge(w_l, 1)
            turns(pe, -1, turn)
            pe.wait_ge(kth_ok, C)
            pe.wait_ge(ktl_ok, C)

            def scores(n, u):
                pe.wait_ge(conv, n + 1)
                p = n & (S - 1)
                ch = bass.ds(((n >> (S.bit_length() - 1)) & (C - 1)) * CH, CH)
                for b in range(PAIR):
                    o = ps_s[:, u, b * CH:(b + 1) * CH]
                    j = bass.ds(p * SW + b * P, P)
                    for s in range(SUB):
                        M.matmul(o[:, s * P:(s + 1) * P],
                                 noedge[:, bass.ds(n & (RING - 1), 1), s, b * P:(b + 1) * P].rearrange("p a j -> p (a j)"),
                                 mask_i[:], start=(s == 0), stop=False, skip_group_check=True)
                    M.matmul(o, kqh[:, 1, j], kqh[:, 0, ch], start=False, stop=False, skip_group_check=True)
                    M.matmul(o, kqh[:, 1, j], kql[:, 0, ch], start=False, stop=False, skip_group_check=True)
                    mm = M.matmul(o, kql[:, 1, j], kqh[:, 0, ch], start=False, stop=True, skip_group_check=True)
                mm.then_inc(s_ps, 1)

            def attend(n, p, u):
                pe.wait_ge(el_ok, n + 1)
                for b in range(PAIR):
                    j = p * PAIR + b
                    for s in range(SUB):
                        w = slice(b * CH + s * P, b * CH + (s + 1) * P)
                        M.matmul(ps_o[:, s, 0:D + 1], e_h[:, u, w], tile(xa, j), start=False, stop=False,
                                 skip_group_check=True)
                        M.matmul(ps_o[:, s, 0:D], e_h[:, u, w], tile(xl, j), start=False, stop=False,
                                 skip_group_check=True)
                        mm = M.matmul(ps_o[:, s, 0:D + 1], e_l[:, u, w], tile(xa, j), start=False, stop=True,
                                      skip_group_check=True)
                mm.then_inc(pv, 1)

            def hidden(m, c, p, dst):
                ch = bass.ds(c * CH, CH)
                f = bass.ds(p * P, P)
                M.matmul(dst, w1h[:, f], x2h[:, ch], start=True, stop=False)
                M.matmul(dst, w1h[:, f], x2l[:, ch], start=False, stop=False)
                M.matmul(dst, w1l[:, f], x2h[:, ch], start=False, stop=True).then_inc(z_ps, 1)

            def project(m, e, u, y=ps_y):
                pe.wait_ge(hl_ok, m + 1)
                if u == 0:
                    M.matmul(y[:], ones3[:], b2_p[:, bass.ds(e * D, D)].unsqueeze(1).broadcast_to([3, SUB, D]),
                             start=True, stop=False, skip_group_check=True)
                d = bass.ds((e * FB + u) * D, D)
                for s in range(SUB):
                    w = slice(s * P, (s + 1) * P)
                    M.matmul(y[:, s, :], h_h[:, u, w], w2h[:, d], start=False, stop=False, skip_group_check=True)
                    M.matmul(y[:, s, :], h_h[:, u, w], w2l[:, d], start=False, stop=False, skip_group_check=True)
                    mm = M.matmul(y[:, s, :], h_l[:, u, w], w2h[:, d], start=False, stop=(u == FB - 1),
                                  skip_group_check=True)
                mm.then_inc(y_ps, 1)

            def transposes(c):
                pe.wait_ge(l2_x, c + 1)
                for s in range(SUB):
                    mm = M.transpose(ps_z[:, s * P:(s + 1) * P], xc[:, 0, s, :], ident[:])
                mm.then_inc(t_ps, 1)

            def gate(c):
                pe.wait_ge(t_l, c + 1)
                for s in range(SUB):
                    mm = M.matmul(ps_z[:, s * E_N:(s + 1) * E_N], xtf[:, s * P:(s + 1) * P], wg[:],
                                  start=True, stop=True)
                mm.then_inc(g_ps, 1)

            def clear():
                for s in range(0, SUB, 2):
                    M.matmul(ps_o[:, s:s + 2, :], zero1[:, 0:P], zero1[:].unsqueeze(1).broadcast_to([1, 2, 2 * D]),
                             start=True, stop=True, skip_group_check=True)

            scores(0, 0)
            scores(1, 1)

            def chunk(c, ffn, last):
                if not ffn:
                    if c > 0:
                        pe.wait_ge(o_free, c)
                    clear()
                    for q, prepare in ((0, None), (MID // QS, transposes), (LATE // QS, gate)):
                        if prepare and c > 0:
                            prepare(c - 1)
                        with pe.Fori(q * QS, (MID, LATE, S)[(q * QS >= MID) + (q * QS >= LATE)] - QS + 1, QS) as p0:
                            for k in range(QS):
                                n = c * S + p0 + k
                                pe.wait_ge(e_ok, n + 1)
                                scores(n + 2, k % 2)
                                attend(n, p0 + k, k % 2)
                    return
                for p in range(S):
                    u, n, m = p % 2, c * S + p, (c - LAG) * B + p
                    if p == MID:
                        pe.wait_ge(t_l, c)
                    elif p == LATE:
                        pe.wait_ge(g_rd, c)
                    hidden(m, c - LAG, p, ps_z[:])
                    if not (last and p >= S - 2):
                        pe.wait_ge(e_ok, n + 1)
                        scores(n + 2, u)
                    if p == 0:
                        pe.wait_ge(o_free, c)
                        clear()
                    elif p == MID - 1:
                        pe.wait_ge(h_ok, m + 1)
                        transposes(c - 1)
                    elif p == LATE - 1:
                        pe.wait_ge(h_ok, m + 1)
                        gate(c - 1)
                    attend(n, p, u)
                    project(m, p // FB, u)
            chunk(0, False, False)
            chunk(1, False, False)
            pe.wait_ge(b2_moved, 48)
            pe.wait_ge(w_h, 4)
            with pe.Fori(LAG, C - 1) as c:
                chunk(c, True, False)
            chunk(C - 1, True, True)

            def blocks(c, e, v):
                for u in range(FB):
                    p = e * FB + u
                    hidden(c * B + p, c, p, ps_s[:, v, u * CH:(u + 1) * CH])

            def outputs(c, e, v):
                for u in range(FB):
                    project(c * B + e * FB + u, e, u, y_of[v])

            def experts(c, lo, hi):
                with pe.Fori(lo, hi - 1, 2) as e0:
                    for v in range(2):
                        blocks(c, e0 + v + 1, 1 - v)
                        outputs(c, e0 + v, v)

            def last_experts(c):
                blocks(c, E_N - 1, 1)
                outputs(c, E_N - 2, 0)
                if c + 1 < C:
                    blocks(c + 1, 0, 0)
                outputs(c, E_N - 1, 1)
            blocks(C - 2, 0, 0)
            experts(C - 2, 0, PREP)
            transposes(C - 1)
            experts(C - 2, PREP, PREP + 2)
            gate(C - 1)
            if PREP + 2 < E_N - 2:
                experts(C - 2, PREP + 2, E_N - 2)
            last_experts(C - 2)
            experts(C - 1, 0, E_N - 2)
            last_experts(C - 1)

        @block.vector
        def _(dve):
            V = nc.vector
            q_rows = T // 4

            def stats(i):
                dve.wait_ge(x_in[i], 16)
                for t in range(i * q_rows, (i + 1) * q_rows):
                    V.bn_stats(st[:, t, :], base[:, t, :])
                dve.drain()
                for t in range(i * q_rows, (i + 1) * q_rows):
                    V.bn_aggr(mv[:, t, :], st[:, t, :])
                dve.drain()
                r = slice(i * q_rows, (i + 1) * q_rows)
                V.tensor_scalar(veps[:, r], mv[:, r, 1], LN_EPS, None, ALU.add).then_inc(st_ok, 1)

            def turn(n, u):
                if exists(n):
                    dve.wait_ge(rn_ok, n + 1)
                    V.scalar_tensor_tensor(kn[:, u].rearrange("p (a d) -> p a d", d=D),
                                           kq_rows[u].rearrange("p (a d) -> p a d", d=D), UNIT_SCALE,
                                           rn[:, u].unsqueeze(2).broadcast_to([P, 2 * SUB, D]),
                                           ALU.mult, ALU.mult).then_inc(kn_ok, 1)
                if exists(n - 1):
                    dve.wait_ge(kt_ps, n)
                    V.tensor_copy(kql[:, :, bass.ds((n - 1) * CH, CH)],
                                  ps_s[:, 1, CH:2 * CH].bitcast(BF16).rearrange("p (k i) -> p k i", k=2)).then_inc(ktl_ok, 1)
                if exists(n + 2):
                    if exists(n):
                        dve.wait_ge(xn_ok, n + 1)
                        dve.wait_ge(xl_ok, n + 1)
                    for s in range(SUB):
                        t = (n + 2) * SUB + s
                        V.tensor_scalar(xc[:, u, s, :], tile(base, t), mv[:, bass.ds(t, 1), 0], rstd[:, bass.ds(t, 1)],
                                        ALU.subtract, ALU.mult)
                    dve.drain().then_inc(xc_ok, 1)
                if isinstance(n, int) and n == -2:
                    stats(2)
                if exists(n):
                    dve.wait_ge(kch_ok, n + 1)
                    V.tensor_tensor(kcl[:, u], kn[:, u], kch[:, u], ALU.subtract).then_inc(kcl_ok, 1)
                if exists(n + 1):
                    dve.wait_ge(sq_ok, n + 2)
                    V.tensor_reduce(ss[:, 1 - u], sq[:, 1 - u].rearrange("p (a d) -> p a d", d=D), AX_X, ALU.add)
                    dve.drain()
                    V.tensor_scalar(ss[:, 1 - u], ss[:, 1 - u], (W_SCALE * COS_EPS) ** 2, None,
                                    ALU.max).then_inc(ss_ok, 1)
                if exists(n + 2):
                    dve.wait_ge(xth_ok, n + 3)
                    V.tensor_tensor(xtl[:, u], ps_z[:], xth[:, u], ALU.subtract).then_inc(xtl_ok, 1)

            stats(0)
            stats(1)
            dve.wait_ge(rs_ok, 1)
            turn(-2, 0)
            dve.wait_ge(w_h, 2)
            V.scalar_tensor_tensor(wkql[:], ps_y[:, 0:2, :].rearrange("p a d -> p (a d)"), W_SCALE, wkqh[:],
                                   ALU.mult, ALU.subtract).then_inc(w_l, 1)
            stats(3)
            turn(-1, 1)
            dve.wait_ge(w_h, 4)
            V.scalar_tensor_tensor(w2l[:], w2_in, W_SCALE, w2h[:], ALU.mult, ALU.subtract).then_inc(w_l, 1)
            V.scalar_tensor_tensor(w1l[:], w1_in[:], W_SCALE, w1h[:], ALU.mult, ALU.subtract).then_inc(w_l, 1)
            dve.wait_ge(rs_ok, 4)
            turns(dve, 0, turn)

            def convert(n, b, q):
                V.tensor_scalar(noedge[:, bass.ds(n & (RING - 1), 1)].rearrange("p a s j -> p (a s) j"),
                                adj_in[:, b, :, q * SW:(q + 1) * SW], 0, None, ALU.is_le).then_inc(conv, 1)

            def low(n, u):
                dve.wait_ge(eh_ok, n + 1)
                V.tensor_tensor(e_l[:, u], e_f[:, u], e_h[:, u], ALU.subtract).then_inc(el_ok, 1)

            def hidden(m, u):
                dve.wait_ge(hh_ok, m + 1)
                V.tensor_tensor(h_l[:, u], h_f[:, u], h_h[:, u], ALU.subtract).then_inc(hl_ok, 1)

            def gather(m, c, e, y=ps_y):
                dve.wait_ge(y_ps, m + 1)
                for s in range(SUB):
                    V.scalar_tensor_tensor(tile(base, c * SUB + s), y[:, s, :],
                                           cw[:, bass.ds(c & 1, 1), s, bass.ds(e, 1)].rearrange("p a e -> p (a e)"),
                                           tile(base, c * SUB + s), ALU.mult, ALU.add)
                dve.drain()

            def finish(c):
                dve.wait_ge(pv, (c + 1) * S)
                V.tensor_scalar(den[:, 0], ps_o[:, :, D], TINY, None, ALU.max)
                V.tensor_scalar(self_w[:], ps_o[:, :, D], 0.0, 0.5, ALU.is_le, ALU.mult)
                dve.drain()
                V.reciprocal(den[:, 1], den[:, 0])
                V.tensor_scalar(self_w[:], self_w[:], 0.5, None, ALU.add)
                dve.drain()
                V.tensor_scalar(den[:, 1], den[:, 1], 0.5, None, ALU.mult)
                dve.drain()
                for s in range(SUB):
                    t = c * SUB + s
                    last = V.scalar_tensor_tensor(tile(base, t), ps_o[:, s, 0:D], den[:, 1, s:s + 1], tile(base, t),
                                                  ALU.mult, ALU.add)
                last.then_inc(o_free, 1)
                dve.drain()

            def residual(c):
                for s in range(SUB):
                    t = c * SUB + s
                    V.scalar_tensor_tensor(tile(base, t), tile(xn, t), self_w[:, s:s + 1], tile(base, t),
                                           ALU.mult, ALU.add)
                dve.drain()

            def second_stats(c):
                for s in range(SUB):
                    V.bn_stats(st[:, s, :], tile(base, c * SUB + s))
                dve.drain()
                for s in range(SUB):
                    V.bn_aggr(mv[:, s, :], st[:, s, :])
                dve.drain()
                V.tensor_scalar(veps[:, 0:SUB], mv[:, 0:SUB, 1], LN_EPS, None, ALU.add).then_inc(l2_st, 1)

            def normalise(c):
                dve.wait_ge(l2_rs, c + 1)
                for s in range(SUB):
                    V.tensor_scalar(xc[:, 0, s, :], tile(base, c * SUB + s), mv[:, s, 0:1], rstd[:, s:s + 1],
                                    ALU.subtract, ALU.mult)
                dve.drain().then_inc(l2_x, 1)

            def transposed(c):
                dve.wait_ge(t_h, c + 1)
                ch = bass.ds(c * CH, CH)
                V.tensor_tensor(x2l[:, ch], ps_z[:], x2h[:, ch], ALU.subtract).then_inc(t_l, 1)

            def read_gate(c):
                dve.wait_ge(g_ps, c + 1)
                V.tensor_tensor(lg[:], ps_z[:, 0:SUB * E_N].rearrange("p (s e) -> p s e", e=E_N),
                                gb[:, 0:1, :].broadcast_to([P, SUB, E_N]), ALU.add).then_inc(g_rd, 1)
                dve.drain()

            def rank_gate(c):
                V.tensor_tensor(lg[:], lg[:], gb[:, 1:2, :].broadcast_to([P, SUB, E_N]), ALU.add)
                dve.drain()
                for s in range(SUB):
                    V.tensor_tensor(diff[:, s], lg[:, s:s + 1, :].broadcast_to([P, E_N, E_N]),
                                    lg[:, s, :].unsqueeze(2).broadcast_to([P, E_N, E_N]), ALU.subtract)
                V.tensor_reduce(top[:, 0], lg[:], AX_X, ALU.max)
                dve.drain()
                for s in range(SUB):
                    V.tensor_tensor(diff[:, s], diff[:, s], least[:], ALU.is_ge)
                V.tensor_tensor(lg[:], lg[:], top[:, 0].unsqueeze(2).broadcast_to([P, SUB, E_N]),
                                ALU.subtract).then_inc(g_d, 1)
                dve.drain()
                V.tensor_reduce(rank[:], diff[:], AX_X, ALU.add)
                dve.drain()

            def weigh(c):
                dve.wait_ge(g_e, c + 1)
                V.scalar_tensor_tensor(rank[:], rank[:], 2.0, pe_[:], ALU.is_lt, ALU.mult)
                dve.drain()
                V.tensor_reduce(top[:, 0], rank[:], AX_X, ALU.add)
                dve.drain()
                V.reciprocal(top[:, 1], top[:, 0])
                dve.drain()
                V.scalar_tensor_tensor(cw[:, bass.ds(c & 1, 1)].rearrange("p a s e -> p (a s) e"), rank[:],
                                       1.0 / W_SCALE, top[:, 1].unsqueeze(2).broadcast_to([P, SUB, E_N]),
                                       ALU.mult, ALU.mult)
                dve.drain()

            for n in range(AHEAD):
                if n == 0:
                    dve.wait_ge(adj_s[0], 16)
                convert(n, 0, n)
            low(0, 0)

            def b2_parts():
                V.tensor_scalar(b2_in[:, 0, :], b2_in[:, 0, :], W_SCALE, None, ALU.mult)
                dve.drain()
                for i in range(3):
                    V.tensor_copy(b2_s[:, i, :], b2_in[:, i, :]).then_inc(b2_ok, 1)
                    dve.wait_ge(b2_ok, 2 * i + 1)
                    if i < 2:
                        V.tensor_tensor(b2_in[:, i + 1, :], b2_in[:, i, :], b2_s[:, i, :], ALU.subtract).then_inc(b2_ok, 1)
                        dve.wait_ge(b2_ok, 2 * i + 2)

            def chunk(c, ffn, last):
                prep = not isinstance(c, int) or c > 0
                for p in range(S):
                    u, n, m = p % 2, c * S + p, (c - LAG) * B + p
                    q, k = p // QS + 1, p % QS
                    if not (last and q == NQ):
                        if k == 0:
                            dve.wait_ge(adj_s[q % 2], (((c * NQ + q) >> 1) + 1) * 16)
                        convert(n + AHEAD, q % 2, k)
                    if ffn:
                        hidden(m, u)
                    if prep and p == MID - 1:
                        transposed(c - 1)
                    if prep and p == LATE - 1:
                        read_gate(c - 1)
                    if not (last and p == S - 1):
                        if prep or p > 0:
                            dve.wait_ge(pv, n)
                        low(n + 1, 1 - u)
                    if p == S - 1:
                        finish(c)
                    if ffn and u == 1:
                        gather(m, c - LAG, p // FB)
                    if prep and p in prepare:
                        prepare[p](c - 1)
                    if not ffn and c == 0 and p == QS:
                        b2_parts()
                if ffn:
                    dve.drain().then_inc(done, 1)
            prepare = {0: residual, 1: second_stats, QS - 1: normalise, LATE: rank_gate, LATE + 2: weigh}
            chunk_loops(dve, chunk)

            def low_parts(c, e):
                for u in range(FB):
                    hidden(c * B + e * FB + u, u)

            def last_of(c, e):
                return c * B + e * FB + FB - 1

            def experts(c, lo, hi):
                with dve.Fori(lo, hi - 1, 2) as e0:
                    for v in range(2):
                        low_parts(c, e0 + v + 1)
                        gather(last_of(c, e0 + v), c, e0 + v, y_of[v])
            low_parts(C - 2, 0)
            residual(C - 1)
            second_stats(C - 1)
            experts(C - 2, 0, PREP - 2)
            normalise(C - 1)
            experts(C - 2, PREP - 2, PREP)
            low_parts(C - 2, PREP + 1)
            transposed(C - 1)
            gather(last_of(C - 2, PREP), C - 2, PREP, y_of[0])
            low_parts(C - 2, PREP + 2)
            gather(last_of(C - 2, PREP + 1), C - 2, PREP + 1, y_of[1])
            read_gate(C - 1)
            rank_gate(C - 1)
            if PREP + 2 < E_N - 2:
                experts(C - 2, PREP + 2, E_N - 2)
            for e in range(E_N - 2, E_N):
                if e + 1 < E_N:
                    low_parts(C - 2, e + 1)
                else:
                    low_parts(C - 1, 0)
                gather(last_of(C - 2, e), C - 2, e, y_of[e % 2])
                if e == E_N - 2:
                    weigh(C - 1)
            dve.drain().then_inc(done, 1)
            experts(C - 1, 0, E_N - 2)
            low_parts(C - 1, E_N - 1)
            gather(last_of(C - 1, E_N - 2), C - 1, E_N - 2, y_of[0])
            gather(last_of(C - 1, E_N - 1), C - 1, E_N - 1, y_of[1])
            dve.drain().then_inc(done, 1)
_INS = ["x", "adj", "L0_gnn_Wq", "L0_gnn_Wk", "L0_ffn_Wg", "L0_ffn_bg", "L0_ffn_bias",
        "L0_ffn_W1", "L0_ffn_b1", "L0_ffn_W2", "L0_ffn_b2"]
_OUTS = [((4096, 128), "float32")]


def kernel(**inputs):
    import numpy as _np
    import concourse.bacc as _bacc
    from concourse import mybir as _mybir
    from concourse.bass_utils import run_bass_kernel_spmd as _run

    nc = _bacc.Bacc("TRN2", target_bir_lowering=False, num_devices=1)
    arrays, args = {}, []
    for name in _INS:
        a = _np.ascontiguousarray(inputs[name])
        arrays[f"in_{name}_dram"] = a
        args.append(nc.dram_tensor(f"in_{name}_dram", a.shape, _mybir.dt.from_np(a.dtype), kind="ExternalInput").ap())
    for i, (shape, dtype) in enumerate(_OUTS):
        dt = _mybir.dt.from_np(_np.dtype(dtype))
        args.append(nc.dram_tensor(f"out_{i}_dram", shape, dt, kind="ExternalOutput").ap())
    gnn_moe_layer(nc, *args)
    r = _run(nc, [arrays], core_ids=[0])
    got = tuple(r.results[0][f"out_{i}_dram"] for i in range(len(_OUTS)))
    return got[0]
```

```python
from contextlib import ExitStack

import concourse.bass as bass
from concourse import mybir

F32 = mybir.dt.float32
F16 = mybir.dt.float16
BF16 = mybir.dt.bfloat16
I32 = mybir.dt.int32
ALU = mybir.AluOpType
ACT = mybir.ActivationFunctionType
AX_X = mybir.AxisListType.X

P = 128
SUB = 4
PAIR = 2
AHEAD = 4
RING = 8
LN_EPS = 1e-5
COS_EPS = 1e-4
W_SCALE = 64.0
UNIT_SCALE = 256.0
MASK = -float(2 ** 30)
TINY = 1e-30
LEAST = 1.2e-38


def gnn_moe_layer(nc, x, adj, Wq, Wk, Wg, bg, bias, W1, b1, W2, b2, out):
    N, D = x.shape
    E_N, _, F = W1.shape
    T = N // P
    CH = SUB * P
    C = N // CH
    SW = PAIR * P
    S = N // SW
    QS = 4
    QW = QS * SW
    NQ = N // QW
    FB = F // P
    B = E_N * FB
    LAG = 2
    MID, LATE = S // 2, 3 * S // 4
    PREP = 4
    FIRST = (0, SUB, 2 * SUB, 4 * SUB, 6 * SUB, T)
    PIECES = 8
    SC = 1.0 / (UNIT_SCALE * UNIT_SCALE)
    assert B == S and D == P and FB == PAIR

    with ExitStack() as ctx:
        def sb(name, shape, dt):
            return ctx.enter_context(nc.sbuf_tensor(name, shape, dt))

        def ps(name, shape, dt):
            return ctx.enter_context(nc.psum_tensor(name, shape, dt))

        def sem(name):
            return ctx.enter_context(nc.semaphore(name))

        base = sb("base", [P, T, D], F32)
        xn = sb("xn", [P, T, D], F32)
        xa = sb("xa", [P, T, D + 1], F16)
        xl = sb("xl", [P, T, D], BF16)
        kqh = sb("kqh", [P, 2, N], F16)
        kql = sb("kql", [P, 2, N], BF16)
        adj_in = sb("adj_in", [P, 2, SUB, QW], I32)
        noedge = sb("noedge", [P, RING, SUB, SW], BF16)
        e_f = sb("e_f", [P, 2, PAIR * CH], F32)
        e_h = sb("e_h", [P, 2, PAIR * CH], F16)
        e_l = sb("e_l", [P, 2, PAIR * CH], BF16)
        w1h = sb("w1h", [P, E_N * F], F16)
        w1l = sb("w1l", [P, E_N * F], BF16)
        w2h = sb("w2h", [P, B * D], F16)
        w2l = sb("w2l", [P, B * D], BF16)
        w1_in = sb("w1_in", [P, E_N * F], F32)
        w2_in = sb("w2_in", [P, B * D], F32)
        wkq_in = sb("wkq_in", [P, 2, D], F32)
        wkqh = sb("wkqh", [P, 2 * D], F16)
        wkql = sb("wkql", [P, 2 * D], BF16)
        wg = sb("wg", [P, E_N], F32)
        wgh = sb("wgh", [P, E_N], F16)
        wgl = sb("wgl", [P, E_N], BF16)
        gb = sb("gb", [P, 2, E_N], F32)
        b1_in = sb("b1_in", [B, P], F32)
        b1c = sb("b1c", [P, B], F32)
        b2_in = sb("b2_in", [E_N, 3, D], F32)
        b2_s = sb("b2_s", [E_N, 3, D], BF16)
        b2_p = sb("b2_p", [3, E_N, D], BF16)
        ones3 = sb("ones3", [3, P], BF16)
        zero1 = sb("zero1", [1, 2 * D], F16)
        ident = sb("ident", [P, P], F32)
        ident_h = sb("ident_h", [P, P], F16)
        ident_b = sb("ident_b", [P, P], BF16)
        mask_i = sb("mask_i", [P, P], BF16)
        half = sb("half", [P, T], F32)
        least = sb("least", [P, E_N, E_N], F32)
        st = sb("st", [P, T, 6], F32)
        mv = sb("mv", [P, T, 2], F32)
        veps = sb("veps", [P, T], F32)
        rstd = sb("rstd", [P, T], F32)
        xc = sb("xc", [P, 2, SUB, D], F32)
        xth = sb("xth", [P, 2, CH], F16)
        xtl = sb("xtl", [P, 2, CH], BF16)
        ss = sb("ss", [P, 2, SUB * 2], F32)
        rn = sb("rn", [P, 2, SUB * 2], F32)
        den = sb("den", [P, 2, SUB], F32)
        self_w = sb("self_w", [P, SUB], F32)
        lg = sb("lg", [P, SUB, E_N], F32)
        diff = sb("diff", [P, SUB, E_N, E_N], F32)
        rank = sb("rank", [P, SUB, E_N], F32)
        top = sb("top", [P, 2, SUB], F32)
        gate_e = sb("gate_e", [P, SUB, E_N], F32)
        cw = sb("cw", [P, 2, SUB, E_N], F32)
        kn, kch, kcl = e_f, e_h, e_l
        sq = noedge[:, AHEAD:].rearrange("p (u r) s j -> p u (r s j)", u=2).bitcast(F32)
        h_f = w1_in[:, 0:2 * CH].rearrange("p (u n) -> p u n", u=2)
        h_h = w1_in[:, 2 * CH:3 * CH].bitcast(F16).rearrange("p (u n) -> p u n", u=2)
        h_l = w1_in[:, 3 * CH:4 * CH].bitcast(BF16).rearrange("p (u n) -> p u n", u=2)
        x2h, x2l = kqh[:, 0, :], kql[:, 0, :]

        ps_s = ps("ps_s", [P, 2, PAIR * CH], F32)
        ps_o = ps("ps_o", [P, SUB, 2 * P], F32)
        ps_z = ps("ps_z", [P, CH], F32)
        ps_y = ps("ps_y", [P, SUB, D], F32)
        kq_rows = [ps_s[:, 0, :], ps_o[:].rearrange("p s d -> p (s d)")]
        unit_t = [ps_y[:].rearrange("p s d -> p (s d)").bitcast(F16), ps_s[:, 1, 0:CH].bitcast(BF16)]
        unit_t_last = [unit_t[0], ps_z[:].bitcast(BF16)]
        y_of = [ps_y[:], ps_o[:, 0:2, :].rearrange("p s (h d) -> p (s h) d", d=D)]

        x_in = [sem(f"x_in{i}") for i in range(4)]
        w_in = sem("w_in")
        gate_in = sem("gate_in")
        wff_in = sem("wff_in")
        adj_s = [sem("adj_in0"), sem("adj_in1")]
        b2_moved = sem("b2_moved")
        out_s = sem("out_s")
        k_set = sem("k_set")
        k_ok = sem("k_ok")
        wt_ps = sem("wt_ps")
        w_h = sem("w_h")
        w_l = sem("w_l")
        wff_h = sem("wff_h")
        b2_ok = sem("b2_ok")
        st_ok = sem("st_ok")
        rs_ok = sem("rs_ok")
        xc_ok = sem("xc_ok")
        xa_ok = sem("xa_ok")
        xn_ok = sem("xn_ok")
        xl_ok = sem("xl_ok")
        xt_ps = sem("xt_ps")
        xth_ok = sem("xth_ok")
        xtl_ok = sem("xtl_ok")
        kq_ps = sem("kq_ps")
        sq_ok = sem("sq_ok")
        ss_ok = sem("ss_ok")
        rn_ok = sem("rn_ok")
        kn_ok = sem("kn_ok")
        kch_ok = sem("kch_ok")
        kcl_ok = sem("kcl_ok")
        last_kcl = sem("last_kcl")
        kt_ps = sem("kt_ps")
        kth_ok = sem("kth_ok")
        ktl_ok = sem("ktl_ok")
        conv = sem("conv")
        s_ps = sem("s_ps")
        e_ok = sem("e_ok")
        eh_ok = sem("eh_ok")
        el_ok = sem("el_ok")
        pv = sem("pv")
        o_free = sem("o_free")
        l2_st = sem("l2_st")
        l2_rs = sem("l2_rs")
        l2_x = sem("l2_x")
        t_ps = sem("t_ps")
        t_h = sem("t_h")
        t_l = sem("t_l")
        g_ps = sem("g_ps")
        g_rd = sem("g_rd")
        g_d = sem("g_d")
        g_e = sem("g_e")
        z_ps = sem("z_ps")
        left_z = sem("left_z")
        h_ok = sem("h_ok")
        hh_ok = sem("hh_ok")
        hl_ok = sem("hl_ok")
        y_ps = sem("y_ps")
        y_free = sem("y_free")
        done = sem("done")

        block = ctx.enter_context(nc.Block())

        def tile(m, t):
            return m[:, bass.ds(t, 1), :].rearrange("p a d -> p (a d)")

        def piece(i, parts):
            k, n = divmod(i, PIECES // 2)
            w = E_N * F // (PIECES // 2)
            return parts[k], (w1_in, w2_in)[k], slice(n * w, (n + 1) * w)

        def exists(n):
            return not isinstance(n, int) or 0 <= n < C

        def draining(n):
            return isinstance(n, int) and n >= C - 3

        def turns(eng, lo, turn):
            for n in range(lo, 1):
                turn(n, n % 2)
            with eng.Fori(1, C - 4, 2) as n1:
                for k in range(2):
                    turn(n1 + k, 1 - k)
            for n in range(C - 3, C):
                turn(n, n % 2)

        @block.sync
        def _(sp):
            for i in range(4):
                n = T // 4
                sp.dma_start(base[:, i * n:(i + 1) * n, :],
                             x.rearrange("(i t p) d -> i p t d", i=4, p=P)[i]).then_inc(x_in[i], 16)
            rows = adj.rearrange("(c s p) (q w) -> c q p s w", s=SUB, p=P, w=QW)

            def load_adj(c, q):
                sp.dma_start(adj_in[:, q % 2], rows[c, q]).then_inc(adj_s[q % 2], 16)
            sp.wait_ge(wff_in, 32)
            for q in range(NQ):
                if q >= 2:
                    sp.wait_ge(conv, QS * (q - 1))
                load_adj(0, q)
            with sp.Fori(1, C) as c:
                for q in range(NQ):
                    sp.wait_ge(conv, c * S + QS * (q - 1))
                    load_adj(c, q)
            with sp.Fori(0, C) as c:
                sp.wait_ge(done, c + 1)
                sp.dma_start(out.rearrange("(c s p) d -> c p s d", s=SUB, p=P)[c],
                             base[:, bass.ds(c * SUB, SUB), :]).then_inc(out_s, 16)
            sp.wait_ge(out_s, 16 * C)

        @block.gpsimd
        def _(pool):
            for m, v in ((ident, 0.0), (ident_h, 0.0), (ident_b, 0.0), (mask_i, 0.0), (half, -0.5),
                         (least, LEAST), (ones3, 1.0), (zero1, 0.0)):
                nc.gpsimd.memset(m[:], v).then_inc(k_set, 1)
            nc.gpsimd.memset(xa[:, :, D:D + 1], 2.0).then_inc(k_set, 1)
            pool.wait_ge(k_set, 9)
            for m, v in ((ident, 1.0), (ident_h, 1.0), (ident_b, 1.0), (mask_i, MASK)):
                nc.gpsimd.affine_select(out=m[:], in_=m[:], compare_op=ALU.not_equal, fill=v, base=0,
                                        pattern=[[-1, P]], channel_multiplier=1).then_inc(k_ok, 1)
            nc.gpsimd.affine_select(out=least[:], in_=least[:], compare_op=ALU.is_ge, fill=0.0, base=0,
                                    pattern=[[-1, E_N], [1, E_N]], channel_multiplier=0).then_inc(k_ok, 1)

            def first_rstd(i):
                pool.wait_ge(st_ok, i + 1)
                r = slice(FIRST[i], FIRST[i + 1])
                nc.gpsimd.tensor_tensor(rstd[:, r], veps[:, r], half[:, r], ALU.pow).then_inc(rs_ok, 1)

            def turn(n, u):
                if exists(n + 2):
                    pool.wait_ge(xa_ok, n + 3)
                    t = bass.ds((n + 2) * SUB, SUB)
                    nc.gpsimd.tensor_tensor(xl[:, t, :], xc[:, u], xa[:, t, 0:D], ALU.subtract).then_inc(xl_ok, 1)
                if exists(n + 1):
                    pool.wait_ge(ss_ok, n + 2)
                    nc.gpsimd.tensor_tensor(rn[:, 1 - u], ss[:, 1 - u], half[:, 0:2 * SUB], ALU.pow).then_inc(rn_ok, 1)
                if exists(n) and not draining(n):
                    pool.wait_ge(kch_ok, n + 1)
                    nc.gpsimd.tensor_tensor(kcl[:, u], kn[:, u], kch[:, u], ALU.subtract).then_inc(kcl_ok, 1)
            first_rstd(0)
            first_rstd(1)
            first_rstd(2)
            turn(-2, 0)
            first_rstd(3)
            turn(-1, 1)
            first_rstd(4)
            turns(pool, 0, turn)
            with pool.Fori(0, C) as c:
                pool.wait_ge(l2_st, c + 1)
                nc.gpsimd.tensor_tensor(rstd[:, 0:SUB], veps[:, 0:SUB], half[:, 0:SUB], ALU.pow).then_inc(l2_rs, 1)

        @block.scalar
        def _(act):
            A = nc.scalar
            for dst, src in ((wkq_in[:, 0, :], Wk), (wkq_in[:, 1, :], Wq),
                             (b1_in[:], b1.rearrange("e (b f) -> (e b) f", f=P))):
                act.dma_start(dst, src).then_inc(w_in, 16)
            for dst, src in ((wg[:], Wg), (b2_in[:, 0, :], b2),
                             (gb[:, 0, :], bg.rearrange("(a e) -> a e", a=1).broadcast_to([P, E_N])),
                             (gb[:, 1, :], bias.rearrange("(a e) -> a e", a=1).broadcast_to([P, E_N]))):
                act.dma_start(dst, src).then_inc(gate_in, 16)
            act.dma_start(w1_in[:].rearrange("p (e f) -> p e f", e=E_N),
                          W1.rearrange("e d f -> d e f")).then_inc(wff_in, 16)
            act.dma_start(w2_in[:].rearrange("p (g d) -> p g d", d=D),
                          W2.rearrange("e (b f) d -> f (e b) d", f=P)).then_inc(wff_in, 16)
            act.wait_ge(wt_ps, 1)
            A.activation(wkqh[:], ps_y[:, 0:2, :].rearrange("p a d -> p (a d)"), ACT.Copy, scale=W_SCALE).then_inc(w_h, 1)
            A.activation(b1c[:], ps_y[:, 2, 0:B], ACT.Copy).then_inc(w_h, 1)

            def turn(n, u):
                if exists(n):
                    act.wait_ge(kn_ok, n + 1)
                    if exists(n - 2):
                        act.wait_ge(kt_ps, n - 1)
                    A.activation(kch[:, u], kn[:, u], ACT.Copy).then_inc(kch_ok, 1)
                if exists(n - 1):
                    act.wait_ge(kt_ps, n)
                    A.activation(kqh[:, :, bass.ds((n - 1) * CH, CH)],
                                 unit_t[0].rearrange("p (k i) -> p k i", k=2), ACT.Copy).then_inc(kth_ok, 1)
                if exists(n + 2):
                    act.wait_ge(kq_ps, n + 3)
                    A.activation(sq[:, u], kq_rows[u], ACT.Square).then_inc(sq_ok, 1)
                if exists(n + 3):
                    t = bass.ds((n + 3) * SUB, SUB)
                    act.wait_ge(xc_ok, n + 4)
                    A.activation(xa[:, t, 0:D], xc[:, 1 - u], ACT.Copy).then_inc(xa_ok, 1)
                    act.wait_ge(xt_ps, n + 4)
                    A.activation(xth[:, 1 - u], ps_z[:], ACT.Copy).then_inc(xth_ok, 1)
                    A.activation(xn[:, t, :], xc[:, 1 - u], ACT.Copy).then_inc(xn_ok, 1)
            turns(act, -3, turn)

            def exps(n, u, between=None):
                act.wait_ge(s_ps, n + 1)
                A.activation(e_f[:, u], ps_s[:, u], ACT.Exp, scale=SC).then_inc(e_ok, 1)
                if between:
                    between()
                act.wait_ge(e_ok, n + 1)
                A.activation(e_h[:, u], e_f[:, u], ACT.Copy).then_inc(eh_ok, 1)

            def hidden(m, p, u):
                act.wait_ge(z_ps, m + 1)
                A.activation(h_f[:, u], ps_z[:], ACT.Relu, scale=1.0 / W_SCALE, bias=b1c[:, bass.ds(p, 1)]).then_inc(h_ok, 1)
                act.wait_ge(h_ok, m + 1)
                A.activation(h_h[:, u], h_f[:, u], ACT.Copy).then_inc(hh_ok, 1)

            def weights_high(i):
                dst, src, r = piece(i, (w1h, w2h))
                if i == 0:
                    act.wait_ge(gate_in, 4 * 16)
                    A.activation(wgh[:], wg[:], ACT.Copy, scale=W_SCALE)
                    act.wait_ge(wff_in, 32)
                A.activation(dst[:, r], src[:, r], ACT.Copy, scale=W_SCALE).then_inc(wff_h, 1)

            def transposed(c):
                act.wait_ge(t_ps, c + 1)
                A.activation(x2h[:, bass.ds(c * CH, CH)], ps_z[:], ACT.Copy).then_inc(t_h, 1)

            def gate(c):
                act.wait_ge(g_d, c + 1)
                A.activation(gate_e[:], lg[:], ACT.Exp).then_inc(g_e, 1)

            exps(0, 0)
            turn(C, 0)

            def chunk(c, ffn, last):
                prep = not isinstance(c, int) or c > 0
                for p in range(S):
                    u, n = p % 2, c * S + p
                    if ffn:
                        hidden((c - LAG) * B + p, p, u)
                    if not (last and p == S - 1):
                        if prep or p > 0:
                            act.wait_ge(el_ok, n)
                            act.wait_ge(pv, n)
                        exps(n + 1, 1 - u, (lambda: transposed(c - 1)) if prep and p == MID - 1 else None)
                    if not prep and 2 <= p < 2 + PIECES:
                        weights_high(p - 2)
                    if prep and p == LATE + 1:
                        gate(c - 1)
                    if not prep and p == S - 1:
                        act.wait_ge(b2_ok, 3)
                        for i in range(3):
                            act.dma_start(b2_p[i:i + 1], b2_s[:, i:i + 1, :]).then_inc(b2_moved, 16)
            chunk(0, False, False)
            chunk(1, False, False)
            with act.Fori(LAG, C - 1) as c:
                chunk(c, True, False)
            chunk(C - 1, True, True)

            for g in range(LAG * E_N):
                c, e, v = C - LAG + g // E_N, g % E_N, g % 2
                if g < 2:
                    act.wait_ge(el_ok, C * S - 1 + g)
                    act.wait_ge(pv, C * S - 1 + g)
                for u in range(FB):
                    p = e * FB + u
                    m, w = c * B + p, slice(u * CH, (u + 1) * CH)
                    act.wait_ge(left_z, g * FB + u + 1)
                    if g >= 2:
                        act.wait_ge(hl_ok, m - 3)
                    A.activation(e_f[:, v, w], ps_s[:, v, w], ACT.Relu, scale=1.0 / W_SCALE,
                                 bias=b1c[:, p:p + 1]).then_inc(h_ok, 1)
                    act.wait_ge(h_ok, m + 1)
                    if g >= 2:
                        act.wait_ge(y_ps, m - 3)
                    A.activation(e_h[:, v, w], e_f[:, v, w], ACT.Copy).then_inc(hh_ok, 1)
                if g == PREP + 1:
                    transposed(C - 1)
                elif g == PREP + 4:
                    gate(C - 1)

        @block.tensor
        def _(pe):
            M = nc.tensor
            pe.wait_ge(k_ok, 5)
            pe.wait_ge(w_in, 3 * 16)
            for k in range(2):
                M.transpose(ps_y[:, k, :], wkq_in[:, k, :], ident[:])
            M.transpose(ps_y[:, 2, 0:B], b1_in[:], ident[0:B, 0:B]).then_inc(wt_ps, 1)

            def scores(n, u):
                pe.wait_ge(conv, n + 1)
                p = n & (S - 1)
                ch = bass.ds(((n >> (S.bit_length() - 1)) & (C - 1)) * CH, CH)
                for b in range(PAIR):
                    o = ps_s[:, u, b * CH:(b + 1) * CH]
                    j = bass.ds(p * SW + b * P, P)
                    for s in range(SUB):
                        M.matmul(o[:, s * P:(s + 1) * P],
                                 noedge[:, bass.ds(n & (RING - 1), 1), s, b * P:(b + 1) * P].rearrange("p a j -> p (a j)"),
                                 mask_i[:], start=(s == 0), stop=False, skip_group_check=True)
                    M.matmul(o, kqh[:, 1, j], kqh[:, 0, ch], start=False, stop=False, skip_group_check=True)
                    M.matmul(o, kqh[:, 1, j], kql[:, 0, ch], start=False, stop=False, skip_group_check=True)
                    mm = M.matmul(o, kql[:, 1, j], kqh[:, 0, ch], start=False, stop=True, skip_group_check=True)
                mm.then_inc(s_ps, 1)

            def turn(n, u):
                if isinstance(n, int) and n == C - 1:
                    pe.wait_ge(kn_ok, C - 1)
                    scores(0, 0)
                if exists(n - 1):
                    if draining(n - 1):
                        pe.wait_ge(last_kcl, n - (C - 3))
                    else:
                        pe.wait_ge(kcl_ok, n)
                    if exists(n - 2):
                        pe.wait_ge(kth_ok, n - 1)
                        pe.wait_ge(ktl_ok, n - 1)
                    hi, lo = unit_t_last if isinstance(n, int) and n == C else unit_t
                    for s in range(SUB):
                        for k in range(2):
                            i = slice((2 * s + k) * D, (2 * s + k + 1) * D)
                            w = slice((k * SUB + s) * P, (k * SUB + s + 1) * P)
                            M.transpose(hi[:, w], kch[:, 1 - u, i], ident_h[:])
                            mm = M.transpose(lo[:, w], kcl[:, 1 - u, i], ident_b[:])
                    mm.then_inc(kt_ps, 1)
                if exists(n + 2):
                    pe.wait_ge(xth_ok, n + 3)
                    pe.wait_ge(xtl_ok, n + 3)
                    for s in range(SUB):
                        o = kq_rows[u][:, s * 2 * D:(s + 1) * 2 * D]
                        t = slice(s * P, (s + 1) * P)
                        M.matmul(o, xth[:, u, t], wkqh[:], start=True, stop=False)
                        M.matmul(o, xth[:, u, t], wkql[:], start=False, stop=False)
                        mm = M.matmul(o, xtl[:, u, t], wkqh[:], start=False, stop=True)
                    mm.then_inc(kq_ps, 1)
                if exists(n + 3):
                    pe.wait_ge(xc_ok, n + 4)
                    for s in range(SUB):
                        mm = M.transpose(ps_z[:, s * P:(s + 1) * P], xc[:, 1 - u, s, :], ident[:])
                    mm.then_inc(xt_ps, 1)

            turn(-3, 1)
            pe.wait_ge(w_h, 1)
            pe.wait_ge(w_l, 1)
            turns(pe, -2, turn)

            def attend(n, p, u):
                pe.wait_ge(el_ok, n + 1)
                for b in range(PAIR):
                    j = p * PAIR + b
                    for s in range(SUB):
                        w = slice(b * CH + s * P, b * CH + (s + 1) * P)
                        M.matmul(ps_o[:, s, 0:D + 1], e_h[:, u, w], tile(xa, j), start=False, stop=False,
                                 skip_group_check=True)
                        M.matmul(ps_o[:, s, 0:D], e_h[:, u, w], tile(xl, j), start=False, stop=False,
                                 skip_group_check=True)
                        mm = M.matmul(ps_o[:, s, 0:D + 1], e_l[:, u, w], tile(xa, j), start=False, stop=True,
                                      skip_group_check=True)
                mm.then_inc(pv, 1)

            def hidden(c, p, dst):
                ch = bass.ds(c * CH, CH)
                f = bass.ds(p * P, P)
                M.matmul(dst, w1h[:, f], x2h[:, ch], start=True, stop=False)
                M.matmul(dst, w1h[:, f], x2l[:, ch], start=False, stop=False)
                return M.matmul(dst, w1l[:, f], x2h[:, ch], start=False, stop=True)

            def project(m, e, u, y=ps_y, parts=(h_h, h_l)):
                pe.wait_ge(hl_ok, m + 1)
                if u == 0:
                    M.matmul(y[:], ones3[:], b2_p[:, bass.ds(e, 1), :].broadcast_to([3, SUB, D]),
                             start=True, stop=False, skip_group_check=True)
                d = bass.ds((e * FB + u) * D, D)
                hi, lo = parts
                for s in range(SUB):
                    w = slice(s * P, (s + 1) * P)
                    M.matmul(y[:, s, :], hi[:, u, w], w2h[:, d], start=False, stop=False, skip_group_check=True)
                    M.matmul(y[:, s, :], hi[:, u, w], w2l[:, d], start=False, stop=False, skip_group_check=True)
                    mm = M.matmul(y[:, s, :], lo[:, u, w], w2h[:, d], start=False, stop=(u == FB - 1),
                                  skip_group_check=True)
                mm.then_inc(y_ps, 1)

            def transposes(c):
                pe.wait_ge(l2_x, c + 1)
                for s in range(SUB):
                    mm = M.transpose(ps_z[:, s * P:(s + 1) * P], xc[:, 0, s, :], ident[:])
                mm.then_inc(t_ps, 1)

            def gate(c):
                pe.wait_ge(t_l, c + 1)
                for s in range(SUB):
                    o = ps_z[:, s * E_N:(s + 1) * E_N]
                    i = bass.ds(c * CH + s * P, P)
                    M.matmul(o, x2h[:, i], wgh[:], start=True, stop=False)
                    M.matmul(o, x2h[:, i], wgl[:], start=False, stop=False)
                    mm = M.matmul(o, x2l[:, i], wgh[:], start=False, stop=True)
                mm.then_inc(g_ps, 1)

            def clear():
                for s in range(0, SUB, 2):
                    M.matmul(ps_o[:, s:s + 2, :], zero1[:, 0:P], zero1[:].unsqueeze(1).broadcast_to([1, 2, 2 * D]),
                             start=True, stop=True, skip_group_check=True)

            def left_blocks(g):
                c, e = C - LAG + g // E_N, g % E_N
                for u in range(FB):
                    p = e * FB + u
                    hidden(c, p, ps_s[:, g % 2, u * CH:(u + 1) * CH]).then_inc(left_z, 1)

            pe.wait_ge(kth_ok, C - 1)
            pe.wait_ge(ktl_ok, C - 1)
            scores(1, 1)
            turn(C, 0)

            def chunk(c, ffn, last):
                prep = not isinstance(c, int) or c > 0
                for p in range(S):
                    u, n, m = p % 2, c * S + p, (c - LAG) * B + p
                    if ffn:
                        if p == MID:
                            pe.wait_ge(t_l, c)
                        elif p == LATE:
                            pe.wait_ge(g_rd, c)
                        hidden(c - LAG, p, ps_z[:]).then_inc(z_ps, 1)
                    if not prep and n + 2 == S - CH // SW:
                        pe.wait_ge(kth_ok, C)
                        pe.wait_ge(ktl_ok, C)
                    if not (last and p >= S - 2):
                        pe.wait_ge(e_ok, n + 1)
                        scores(n + 2, u)
                    if p == 0:
                        if prep:
                            pe.wait_ge(o_free, c)
                        clear()
                    elif prep and p == MID - 1:
                        if ffn:
                            pe.wait_ge(h_ok, m + 1)
                        transposes(c - 1)
                    elif prep and p == LATE - 1:
                        if ffn:
                            pe.wait_ge(h_ok, m + 1)
                        gate(c - 1)
                    elif last and p >= S - 2:
                        pe.wait_ge(e_ok, n + 1)
                        left_blocks(p - (S - 2))
                    attend(n, p, u)
                    if ffn:
                        if p == 0:
                            pe.wait_ge(y_free, c - 1)
                        project(m, p // FB, u)
            chunk(0, False, False)
            chunk(1, False, False)
            pe.wait_ge(b2_moved, 48)
            pe.wait_ge(wff_h, PIECES)
            pe.wait_ge(w_l, 1 + PIECES)
            with pe.Fori(LAG, C - 1) as c:
                chunk(c, True, False)
            chunk(C - 1, True, True)

            for g in range(LAG * E_N):
                c, e, v = C - LAG + g // E_N, g % E_N, g % 2
                if g + 2 < LAG * E_N:
                    pe.wait_ge(h_ok, (C - LAG) * B + (g + 1) * FB)
                    left_blocks(g + 2)
                if g == 0:
                    pe.wait_ge(y_free, C - 1)
                elif g == 1:
                    pe.wait_ge(o_free, C)
                parts = [m[:, v, :].rearrange("p (u n) -> p u n", u=2) for m in (e_h, e_l)]
                for u in range(FB):
                    project(c * B + e * FB + u, e, u, y_of[v], parts)
                if g == PREP:
                    transposes(C - 1)
                elif g == PREP + 1:
                    gate(C - 1)

        @block.vector
        def _(dve):
            V = nc.vector

            def stats(i):
                tiles = range(FIRST[i], FIRST[i + 1])
                dve.wait_ge(x_in[tiles[-1] // (T // 4)], 16)
                for t in tiles:
                    V.bn_stats(st[:, t, :], base[:, t, :])
                dve.drain()
                for t in tiles:
                    V.bn_aggr(mv[:, t, :], st[:, t, :])
                dve.drain()
                r = slice(FIRST[i], FIRST[i + 1])
                V.tensor_scalar(veps[:, r], mv[:, r, 1], LN_EPS, None, ALU.add).then_inc(st_ok, 1)

            def convert(n, b, q):
                V.tensor_scalar(noedge[:, bass.ds(n & (RING - 1), 1)].rearrange("p a s j -> p (a s) j"),
                                adj_in[:, b, :, q * SW:(q + 1) * SW], 0, None, ALU.is_le).then_inc(conv, 1)

            def kcl_of(n, u):
                dve.wait_ge(kch_ok, n + 1)
                V.tensor_tensor(kcl[:, u], kn[:, u], kch[:, u], ALU.subtract).then_inc(last_kcl, 1)
                if n > C - 3:
                    convert(n - (C - 3) + 1, 0, n - (C - 3) + 1)

            def turn(n, u):
                if exists(n):
                    dve.wait_ge(rn_ok, n + 1)
                    V.scalar_tensor_tensor(kn[:, u].rearrange("p (a d) -> p a d", d=D),
                                           kq_rows[u].rearrange("p (a d) -> p a d", d=D), UNIT_SCALE,
                                           rn[:, u].unsqueeze(2).broadcast_to([P, 2 * SUB, D]),
                                           ALU.mult, ALU.mult).then_inc(kn_ok, 1)
                if exists(n + 1):
                    dve.wait_ge(sq_ok, n + 2)
                    V.tensor_reduce(ss[:, 1 - u], sq[:, 1 - u].rearrange("p (a d) -> p a d", d=D), AX_X, ALU.add)
                    dve.drain()
                    V.tensor_scalar(ss[:, 1 - u], ss[:, 1 - u], (W_SCALE * COS_EPS) ** 2, None,
                                    ALU.max).then_inc(ss_ok, 1)
                if exists(n + 2):
                    dve.wait_ge(xth_ok, n + 3)
                    V.tensor_tensor(xtl[:, u], ps_z[:], xth[:, u], ALU.subtract).then_inc(xtl_ok, 1)
                if exists(n + 3):
                    if exists(n + 1):
                        dve.wait_ge(xn_ok, n + 2)
                        dve.wait_ge(xl_ok, n + 2)
                    for s in range(SUB):
                        t = (n + 3) * SUB + s
                        V.tensor_scalar(xc[:, 1 - u, s, :], tile(base, t), mv[:, bass.ds(t, 1), 0],
                                        rstd[:, bass.ds(t, 1)], ALU.subtract, ALU.mult)
                    dve.drain().then_inc(xc_ok, 1)
                if draining(n) and n < C - 1:
                    kcl_of(n, u)
                if exists(n - 1):
                    dve.wait_ge(kt_ps, n)
                    lo = (unit_t_last if isinstance(n, int) and n == C else unit_t)[1]
                    V.tensor_copy(kql[:, :, bass.ds((n - 1) * CH, CH)],
                                  lo.rearrange("p (k i) -> p k i", k=2)).then_inc(ktl_ok, 1)
                if draining(n) and n == C - 1:
                    kcl_of(n, u)

            stats(0)
            stats(1)
            dve.wait_ge(rs_ok, 1)
            turn(-3, 1)
            stats(2)
            dve.wait_ge(w_h, 2)
            V.scalar_tensor_tensor(wkql[:], ps_y[:, 0:2, :].rearrange("p a d -> p (a d)"), W_SCALE, wkqh[:],
                                   ALU.mult, ALU.subtract).then_inc(w_l, 1)
            dve.wait_ge(rs_ok, 2)
            turn(-2, 0)
            stats(3)
            dve.wait_ge(rs_ok, 3)
            turn(-1, 1)
            stats(4)
            turn(0, 0)
            dve.wait_ge(adj_s[0], 16)
            convert(0, 0, 0)
            convert(1, 0, 1)
            dve.wait_ge(rs_ok, 5)
            turns(dve, 1, turn)

            def low(n, u):
                dve.wait_ge(eh_ok, n + 1)
                V.tensor_tensor(e_l[:, u], e_f[:, u], e_h[:, u], ALU.subtract).then_inc(el_ok, 1)

            def hidden(m, u):
                dve.wait_ge(hh_ok, m + 1)
                V.tensor_tensor(h_l[:, u], h_f[:, u], h_h[:, u], ALU.subtract).then_inc(hl_ok, 1)

            def gather(m, c, e, y=ps_y):
                dve.wait_ge(y_ps, m + 1)
                for s in range(SUB):
                    V.scalar_tensor_tensor(tile(base, c * SUB + s), y[:, s, :],
                                           cw[:, bass.ds(c & 1, 1), s, bass.ds(e, 1)].rearrange("p a e -> p (a e)"),
                                           tile(base, c * SUB + s), ALU.mult, ALU.add)
                dve.drain()

            def finish(c):
                dve.wait_ge(pv, (c + 1) * S)
                V.tensor_scalar(den[:, 0], ps_o[:, :, D], TINY, None, ALU.max)
                dve.drain()
                V.reciprocal(den[:, 1], den[:, 0])
                V.tensor_scalar(self_w[:], ps_o[:, :, D], 0.0, 0.5, ALU.is_le, ALU.mult)
                dve.drain()
                for s in range(SUB):
                    t = c * SUB + s
                    last = V.scalar_tensor_tensor(tile(base, t), ps_o[:, s, 0:D], den[:, 1, s:s + 1], tile(base, t),
                                                  ALU.mult, ALU.add)
                last.then_inc(o_free, 1)

            def residual(c):
                V.tensor_scalar(self_w[:], self_w[:], 0.5, None, ALU.add)
                dve.drain()
                for s in range(SUB):
                    t = c * SUB + s
                    V.scalar_tensor_tensor(tile(base, t), tile(xn, t), self_w[:, s:s + 1], tile(base, t),
                                           ALU.mult, ALU.add)
                dve.drain()

            def second_stats(c):
                for s in range(SUB):
                    V.bn_stats(st[:, s, :], tile(base, c * SUB + s))
                dve.drain()
                for s in range(SUB):
                    V.bn_aggr(mv[:, s, :], st[:, s, :])
                dve.drain()
                V.tensor_scalar(veps[:, 0:SUB], mv[:, 0:SUB, 1], LN_EPS, None, ALU.add).then_inc(l2_st, 1)

            def normalise(c):
                dve.wait_ge(l2_rs, c + 1)
                for s in range(SUB):
                    V.tensor_scalar(xc[:, 0, s, :], tile(base, c * SUB + s), mv[:, s, 0:1], rstd[:, s:s + 1],
                                    ALU.subtract, ALU.mult)
                dve.drain().then_inc(l2_x, 1)

            def transposed(c):
                dve.wait_ge(t_h, c + 1)
                ch = bass.ds(c * CH, CH)
                V.tensor_tensor(x2l[:, ch], ps_z[:], x2h[:, ch], ALU.subtract).then_inc(t_l, 1)

            def read_gate(c):
                dve.wait_ge(g_ps, c + 1)
                V.scalar_tensor_tensor(lg[:], ps_z[:, 0:SUB * E_N].rearrange("p (s e) -> p s e", e=E_N),
                                       1.0 / W_SCALE, gb[:, 0:1, :].broadcast_to([P, SUB, E_N]),
                                       ALU.mult, ALU.add).then_inc(g_rd, 1)
                dve.drain()

            def rank_gate(c):
                V.tensor_tensor(lg[:], lg[:], gb[:, 1:2, :].broadcast_to([P, SUB, E_N]), ALU.add)
                dve.drain()
                for s in range(SUB):
                    V.tensor_tensor(diff[:, s], lg[:, s:s + 1, :].broadcast_to([P, E_N, E_N]),
                                    lg[:, s, :].unsqueeze(2).broadcast_to([P, E_N, E_N]), ALU.subtract)
                V.tensor_reduce(top[:, 0], lg[:], AX_X, ALU.max)
                dve.drain()
                for s in range(SUB):
                    V.tensor_tensor(diff[:, s], diff[:, s], least[:], ALU.is_ge)
                V.tensor_tensor(lg[:], lg[:], top[:, 0].unsqueeze(2).broadcast_to([P, SUB, E_N]),
                                ALU.subtract).then_inc(g_d, 1)
                dve.drain()
                V.tensor_reduce(rank[:], diff[:], AX_X, ALU.add)
                dve.drain()

            def weigh(c):
                dve.wait_ge(g_e, c + 1)
                V.scalar_tensor_tensor(rank[:], rank[:], 2.0, gate_e[:], ALU.is_lt, ALU.mult)
                dve.drain()
                V.tensor_reduce(top[:, 0], rank[:], AX_X, ALU.add)
                dve.drain()
                V.reciprocal(top[:, 1], top[:, 0])
                dve.drain()
                V.scalar_tensor_tensor(cw[:, bass.ds(c & 1, 1)].rearrange("p a s e -> p (a s) e"), rank[:],
                                       1.0 / W_SCALE, top[:, 1].unsqueeze(2).broadcast_to([P, SUB, E_N]),
                                       ALU.mult, ALU.mult)
                dve.drain()

            low(0, 0)
            turn(C, 0)

            def b2_part(i):
                if i == 0:
                    V.tensor_scalar(b2_in[:, 0, :], b2_in[:, 0, :], W_SCALE, None, ALU.mult)
                    dve.drain()
                V.tensor_copy(b2_s[:, i, :], b2_in[:, i, :]).then_inc(b2_ok, 1)
                if i < 2:
                    dve.wait_ge(b2_ok, i + 1)
                    V.tensor_tensor(b2_in[:, i + 1, :], b2_in[:, i, :], b2_s[:, i, :], ALU.subtract)
                    dve.drain()

            def left_low(g):
                v = g % 2
                for u in range(FB):
                    w = slice(u * CH, (u + 1) * CH)
                    dve.wait_ge(hh_ok, (C - LAG) * B + g * FB + u + 1)
                    V.tensor_tensor(e_l[:, v, w], e_f[:, v, w], e_h[:, v, w], ALU.subtract).then_inc(hl_ok, 1)

            def left_gather(g):
                gather((C - LAG) * B + g * FB + FB - 1, C - LAG + g // E_N, g % E_N, y_of[g % 2])

            def weights_low(i):
                (dst, hi), src, r = piece(i, ((w1l, w1h), (w2l, w2h)))
                dve.wait_ge(wff_h, i + 1)
                if i == 0:
                    V.scalar_tensor_tensor(wgl[:], wg[:], W_SCALE, wgh[:], ALU.mult, ALU.subtract)
                V.scalar_tensor_tensor(dst[:, r], src[:, r], W_SCALE, hi[:, r], ALU.mult, ALU.subtract).then_inc(w_l, 1)

            prepare = {0: residual, 2: second_stats, 4: normalise, LATE: rank_gate, LATE + 2: weigh}

            def chunk(c, ffn, last, carried=True):
                prep = not isinstance(c, int) or c > 0
                for p in range(S):
                    u, n, m = p % 2, c * S + p, (c - LAG) * B + p
                    q, k = p // QS + 1, p % QS
                    if ffn:
                        hidden(m, u)
                    if ffn and p == 0:
                        if carried:
                            gather(m - 1, c - LAG - 1, E_N - 1)
                        dve.drain().then_inc(y_free, 1)
                        if carried:
                            dve.drain().then_inc(done, 1)
                    if prep and p == MID - 1:
                        transposed(c - 1)
                    if prep and p == LATE - 1:
                        read_gate(c - 1)
                    if not (last and q == NQ):
                        if k == 0:
                            dve.wait_ge(adj_s[q % 2], (((c * NQ + q) >> 1) + 1) * 16)
                        convert(n + AHEAD, q % 2, k)
                    if not (last and p == S - 1):
                        if prep or p > 0:
                            dve.wait_ge(pv, n)
                        low(n + 1, 1 - u)
                    if last and p == S - 1:
                        left_low(0)
                    elif p == S - 1:
                        finish(c)
                    if ffn and u == 1 and (last or p < S - 1):
                        gather(m, c - LAG, p // FB)
                    if prep and p in prepare:
                        prepare[p](c - 1)
                    if not prep and 3 <= p < 3 + PIECES:
                        weights_low(p - 3)
                    if not prep and LATE <= p < LATE + 3:
                        b2_part(p - LATE)
                if last:
                    dve.drain().then_inc(y_free, 1)
                    dve.drain().then_inc(done, 1)
                    left_low(1)
                    finish(c)
            chunk(0, False, False)
            chunk(1, False, False)
            chunk(LAG, True, False, carried=False)
            with dve.Fori(LAG + 1, C - 1) as c:
                chunk(c, True, False)
            chunk(C - 1, True, True)

            for g in range(LAG * E_N):
                if 1 < g + 1 < LAG * E_N:
                    left_low(g + 1)
                if g == PREP:
                    transposed(C - 1)
                elif g == PREP + 4:
                    weigh(C - 1)
                left_gather(g)
                if g == 0:
                    residual(C - 1)
                elif g == 1:
                    second_stats(C - 1)
                elif g == 2:
                    normalise(C - 1)
                elif g == PREP + 1:
                    read_gate(C - 1)
                elif g == PREP + 2:
                    rank_gate(C - 1)
                if g % E_N == E_N - 1:
                    dve.drain().then_inc(done, 1)
_INS = ["x", "adj", "L0_gnn_Wq", "L0_gnn_Wk", "L0_ffn_Wg", "L0_ffn_bg", "L0_ffn_bias",
        "L0_ffn_W1", "L0_ffn_b1", "L0_ffn_W2", "L0_ffn_b2"]
_OUTS = [((4096, 128), "float32")]


def kernel(**inputs):
    import numpy as _np
    import concourse.bacc as _bacc
    from concourse import mybir as _mybir
    from concourse.bass_utils import run_bass_kernel_spmd as _run

    nc = _bacc.Bacc("TRN2", target_bir_lowering=False, num_devices=1)
    arrays, args = {}, []
    for name in _INS:
        a = _np.ascontiguousarray(inputs[name])
        arrays[f"in_{name}_dram"] = a
        args.append(nc.dram_tensor(f"in_{name}_dram", a.shape, _mybir.dt.from_np(a.dtype), kind="ExternalInput").ap())
    for i, (shape, dtype) in enumerate(_OUTS):
        dt = _mybir.dt.from_np(_np.dtype(dtype))
        args.append(nc.dram_tensor(f"out_{i}_dram", shape, dt, kind="ExternalOutput").ap())
    gnn_moe_layer(nc, *args)
    r = _run(nc, [arrays], core_ids=[0])
    got = tuple(r.results[0][f"out_{i}_dram"] for i in range(len(_OUTS)))
    return got[0]
```
